# Optimizing a Trainium2 kernel written in Bass

```python
import numpy as np
import jax
import jax.numpy as jnp

def _softmax(x, axis=-1):
    return jax.nn.softmax(x, axis=axis)

def _gelu(x):
    return jax.nn.gelu(x, approximate=True)

def _silu(x):
    return jax.nn.silu(x)

def _sigmoid(x):
    return jax.nn.sigmoid(x)

def _layernorm(x, axis=-1, eps=1e-05):
    m = jnp.mean(x, axis=axis, keepdims=True)
    v = jnp.var(x, axis=axis, keepdims=True)
    return (x - m) / jnp.sqrt(v + eps)

def _scatter_add(tgt, idx, src, axis=0):
    return tgt.at[idx].add(src)

def _segment_sum(src, seg, n):
    return jax.ops.segment_sum(src, seg, n)
kernel_name = 'mk_xattn_seq_d2_seqx_r4_f786ad'

def setup_inputs(seed: int=0):
    np.random.seed(seed)
    _w = jnp.asarray

    def _rec_inputs():
        import jax
        import jax.numpy as jnp
        _rk = jax.random.key(seed)
        x = 7.22e-05 + 1 * jax.random.normal(jax.random.fold_in(_rk, 1), (16, 112, 256), jnp.float32)
        _lenS = 112 - jax.random.randint(jax.random.fold_in(_rk, 7), (16,), 0, max(1, 112 // 4) + 1, jnp.int32)
        _lenS2 = 375 - jax.random.randint(jax.random.fold_in(_rk, 8), (16,), 0, max(1, 375 // 4) + 1, jnp.int32)
        _ctx_768P = jax.random.normal(jax.random.fold_in(_rk, 11), (16, 16, 192), jnp.float32)
        _ctx_768c = jax.random.dirichlet(jax.random.fold_in(_rk, 511), 0.3 * jnp.ones((16,), jnp.float32), (16, 375))
        _ctx_768t = jnp.einsum('bsk,bkd->bsd', _ctx_768c, _ctx_768P)
        _ctx_768t = _ctx_768t * jax.lax.rsqrt(jnp.mean(jnp.square(_ctx_768t)) + 1e-12) * 0.953939
        ctx_768 = 0.000651243 + 0.998673 * (_ctx_768t + 0.3 * jax.random.normal(jax.random.fold_in(_rk, 611), (16, 375, 192), jnp.float32))
        return (x, ctx_768)
    x, ctx_768 = _rec_inputs()

    def _L0_xattn_setup():
        import jax, jax.numpy as jnp
        import numpy as np
        HEADS = 16
        D_HEAD = 64
        EPS = 1e-05

        def _ln(x, g, b):
            m = jnp.mean(x, axis=-1, keepdims=True)
            v = jnp.var(x, axis=-1, keepdims=True)
            return (x - m) * jax.lax.rsqrt(v + EPS) * g + b

        def _attn(xq, xc, Wq, Wk, Wv, Wo, bo):
            B, N, _ = xq.shape
            S = xc.shape[1]
            q = (xq @ Wq).reshape(B, N, HEADS, D_HEAD)
            k = (xc @ Wk).reshape(B, S, HEADS, D_HEAD)
            v = (xc @ Wv).reshape(B, S, HEADS, D_HEAD)
            scale = D_HEAD ** (-0.5)
            scores = jnp.einsum('bnhd,bshd->bhns', q, k) * scale
            attn = jax.nn.softmax(scores, axis=-1)
            out = jnp.einsum('bhns,bshd->bnhd', attn, v).reshape(B, N, HEADS * D_HEAD)
            return out @ Wo + bo

        def _geglu_ff(x, Wp, bp, Wf, bf):
            h = x @ Wp + bp
            a, gate = jnp.split(h, 2, axis=-1)
            return a * jax.nn.gelu(gate, approximate=False) @ Wf + bf
        key = jax.random.key(seed)
        ks = jax.random.split(key, 16)
        dim, ctx, inner, ffin = (256, 192, HEADS * D_HEAD, 4 * 256)

        def w(k, i, o):
            return jax.random.normal(k, (i, o), jnp.float32) * i ** (-0.5)
        inp = {'x': jax.random.normal(ks[0], (4, 512, dim), jnp.float32), 'context': jax.random.normal(ks[1], (4, 77, ctx), jnp.float32), 'Wq1': w(ks[2], dim, inner), 'Wk1': w(ks[3], dim, inner), 'Wv1': w(ks[4], dim, inner), 'Wo1': w(ks[5], inner, dim), 'bo1': jnp.zeros((dim,), jnp.float32), 'Wq2': w(ks[6], dim, inner), 'Wk2': w(ks[7], ctx, inner), 'Wv2': w(ks[8], ctx, inner), 'Wo2': w(ks[9], inner, dim), 'bo2': jnp.zeros((dim,), jnp.float32), 'Wp': w(ks[10], dim, 2 * ffin), 'bp': jnp.zeros((2 * ffin,), jnp.float32), 'Wf': w(ks[11], ffin, dim), 'bf': jnp.zeros((dim,), jnp.float32), 'g1': jnp.ones((dim,), jnp.float32), 'b1': jnp.zeros((dim,), jnp.float32), 'g2': jnp.ones((dim,), jnp.float32), 'b2': jnp.zeros((dim,), jnp.float32), 'g3': jnp.ones((dim,), jnp.float32), 'b3': jnp.zeros((dim,), jnp.float32)}
        return inp
    _L0_xattn_all = _L0_xattn_setup()
    _L0_xattn_in = {k: v for k, v in _L0_xattn_all.items() if k in ('Wq1', 'Wk1', 'Wv1', 'Wo1', 'bo1', 'Wq2', 'Wk2', 'Wv2', 'Wo2', 'bo2', 'Wp', 'bp', 'Wf', 'bf', 'g1', 'b1', 'g2', 'b2', 'g3', 'b3')}
    del _L0_xattn_all

    def _L1_xattn_setup():
        import jax, jax.numpy as jnp
        import numpy as np
        LATENT = 256
        TEXT = 192
        HEADS = 16
        HEAD_DIM = LATENT // HEADS
        SCALE = HEAD_DIM ** (-0.5)
        LN_EPS = 1e-05
        key = jax.random.key(seed)
        ks = jax.random.split(key, 16)
        B, Tx, Txf = (4, 1024, 64)

        def lin(k, fan_in, fan_out):
            bound = 1.0 / np.sqrt(fan_in)
            kw, kb = jax.random.split(k)
            W = jax.random.uniform(kw, (fan_in, fan_out), jnp.float32, -bound, bound)
            b = jax.random.uniform(kb, (fan_out,), jnp.float32, -bound, bound)
            return (W, b)
        Wq, bq = lin(ks[0], LATENT, LATENT)
        Wk, bk = lin(ks[1], TEXT, LATENT)
        Wv, bv = lin(ks[2], TEXT, LATENT)
        Wo, bo = lin(ks[3], LATENT, LATENT)
        W1, b1 = lin(ks[4], LATENT, 4 * LATENT)
        W2, b2 = lin(ks[5], 4 * LATENT, LATENT)
        return {'x': jax.random.normal(ks[6], (B, Tx, LATENT), jnp.float32), 'xf': jax.random.normal(ks[7], (B, Txf, TEXT), jnp.float32), 'Wq': Wq, 'bq': bq, 'Wk': Wk, 'bk': bk, 'Wv': Wv, 'bv': bv, 'Wo': Wo, 'bo': bo, 'ln_g': jnp.ones((LATENT,), jnp.float32), 'ln_b': jnp.zeros((LATENT,), jnp.float32), 'W1': W1, 'b1': b1, 'W2': W2, 'b2': b2}
    _L1_xattn_all = _L1_xattn_setup()
    _L1_xattn_in = {k: v for k, v in _L1_xattn_all.items() if k in ('Wq', 'bq', 'Wk', 'bk', 'Wv', 'bv', 'Wo', 'bo', 'ln_g', 'ln_b', 'W1', 'b1', 'W2', 'b2')}
    del _L1_xattn_all
    return {'x': x, 'ctx_768': ctx_768, 'L0_xattn_Wq1': _L0_xattn_in['Wq1'], 'L0_xattn_Wk1': _L0_xattn_in['Wk1'], 'L0_xattn_Wv1': _L0_xattn_in['Wv1'], 'L0_xattn_Wo1': _L0_xattn_in['Wo1'], 'L0_xattn_bo1': _L0_xattn_in['bo1'], 'L0_xattn_Wq2': _L0_xattn_in['Wq2'], 'L0_xattn_Wk2': _L0_xattn_in['Wk2'], 'L0_xattn_Wv2': _L0_xattn_in['Wv2'], 'L0_xattn_Wo2': _L0_xattn_in['Wo2'], 'L0_xattn_bo2': _L0_xattn_in['bo2'], 'L0_xattn_Wp': _L0_xattn_in['Wp'], 'L0_xattn_bp': _L0_xattn_in['bp'], 'L0_xattn_Wf': _L0_xattn_in['Wf'], 'L0_xattn_bf': _L0_xattn_in['bf'], 'L0_xattn_g1': _L0_xattn_in['g1'], 'L0_xattn_b1': _L0_xattn_in['b1'], 'L0_xattn_g2': _L0_xattn_in['g2'], 'L0_xattn_b2': _L0_xattn_in['b2'], 'L0_xattn_g3': _L0_xattn_in['g3'], 'L0_xattn_b3': _L0_xattn_in['b3'], 'L1_xattn_Wq': _L1_xattn_in['Wq'], 'L1_xattn_bq': _L1_xattn_in['bq'], 'L1_xattn_Wk': _L1_xattn_in['Wk'], 'L1_xattn_bk': _L1_xattn_in['bk'], 'L1_xattn_Wv': _L1_xattn_in['Wv'], 'L1_xattn_bv': _L1_xattn_in['bv'], 'L1_xattn_Wo': _L1_xattn_in['Wo'], 'L1_xattn_bo': _L1_xattn_in['bo'], 'L1_xattn_ln_g': _L1_xattn_in['ln_g'], 'L1_xattn_ln_b': _L1_xattn_in['ln_b'], 'L1_xattn_W1': _L1_xattn_in['W1'], 'L1_xattn_b1': _L1_xattn_in['b1'], 'L1_xattn_W2': _L1_xattn_in['W2'], 'L1_xattn_b2': _L1_xattn_in['b2']}

def reference(x, ctx_768, L0_xattn_Wq1, L0_xattn_Wk1, L0_xattn_Wv1, L0_xattn_Wo1, L0_xattn_bo1, L0_xattn_Wq2, L0_xattn_Wk2, L0_xattn_Wv2, L0_xattn_Wo2, L0_xattn_bo2, L0_xattn_Wp, L0_xattn_bp, L0_xattn_Wf, L0_xattn_bf, L0_xattn_g1, L0_xattn_b1, L0_xattn_g2, L0_xattn_b2, L0_xattn_g3, L0_xattn_b3, L1_xattn_Wq, L1_xattn_bq, L1_xattn_Wk, L1_xattn_bk, L1_xattn_Wv, L1_xattn_bv, L1_xattn_Wo, L1_xattn_bo, L1_xattn_ln_g, L1_xattn_ln_b, L1_xattn_W1, L1_xattn_b1, L1_xattn_W2, L1_xattn_b2):
    import jax
    import jax.numpy as jnp

    def _L0_xattn_ref(x, context, Wq1, Wk1, Wv1, Wo1, bo1, Wq2, Wk2, Wv2, Wo2, bo2, Wp, bp, Wf, bf, g1, b1, g2, b2, g3, b3):
        import jax, jax.numpy as jnp
        import numpy as np
        HEADS = 16
        D_HEAD = 64
        EPS = 1e-05

        def _ln(x, g, b):
            m = jnp.mean(x, axis=-1, keepdims=True)
            v = jnp.var(x, axis=-1, keepdims=True)
            return (x - m) * jax.lax.rsqrt(v + EPS) * g + b

        def _attn(xq, xc, Wq, Wk, Wv, Wo, bo):
            B, N, _ = xq.shape
            S = xc.shape[1]
            q = (xq @ Wq).reshape(B, N, HEADS, D_HEAD)
            k = (xc @ Wk).reshape(B, S, HEADS, D_HEAD)
            v = (xc @ Wv).reshape(B, S, HEADS, D_HEAD)
            scale = D_HEAD ** (-0.5)
            scores = jnp.einsum('bnhd,bshd->bhns', q, k) * scale
            attn = jax.nn.softmax(scores, axis=-1)
            out = jnp.einsum('bhns,bshd->bnhd', attn, v).reshape(B, N, HEADS * D_HEAD)
            return out @ Wo + bo

        def _geglu_ff(x, Wp, bp, Wf, bf):
            h = x @ Wp + bp
            a, gate = jnp.split(h, 2, axis=-1)
            return a * jax.nn.gelu(gate, approximate=False) @ Wf + bf
        x = _attn(_ln(x, g1, b1), _ln(x, g1, b1), Wq1, Wk1, Wv1, Wo1, bo1) + x
        x = _attn(_ln(x, g2, b2), context, Wq2, Wk2, Wv2, Wo2, bo2) + x
        x = _geglu_ff(_ln(x, g3, b3), Wp, bp, Wf, bf) + x
        return x

    def _L1_xattn_ref(x, xf, Wq, bq, Wk, bk, Wv, bv, Wo, bo, ln_g, ln_b, W1, b1, W2, b2):
        import jax, jax.numpy as jnp
        import numpy as np
        LATENT = 256
        TEXT = 192
        HEADS = 16
        HEAD_DIM = LATENT // HEADS
        SCALE = HEAD_DIM ** (-0.5)
        LN_EPS = 1e-05
        B, Tx, D = x.shape
        Txf = xf.shape[1]
        q = (x @ Wq + bq).reshape(B, Tx, HEADS, HEAD_DIM).transpose(0, 2, 1, 3)
        k = (xf @ Wk + bk).reshape(B, Txf, HEADS, HEAD_DIM).transpose(0, 2, 1, 3)
        v = (xf @ Wv + bv).reshape(B, Txf, HEADS, HEAD_DIM).transpose(0, 2, 1, 3)
        scores = jnp.einsum('bhqd,bhkd->bhqk', q * SCALE, k)
        probs = jax.nn.softmax(scores, axis=-1)
        attn = jnp.einsum('bhqk,bhkd->bhqd', probs, v)
        out = attn.transpose(0, 2, 1, 3).reshape(B, Tx, D)
        out = out @ Wo + bo
        mu = jnp.mean(out, axis=-1, keepdims=True)
        var = jnp.var(out, axis=-1, keepdims=True)
        h = (out - mu) * jax.lax.rsqrt(var + LN_EPS) * ln_g + ln_b
        h = jax.nn.gelu(h @ W1 + b1, approximate=False)
        ffn = h @ W2 + b2
        out = out + ffn
        return x + out
    x = _L0_xattn_ref(x, ctx_768, L0_xattn_Wq1, L0_xattn_Wk1, L0_xattn_Wv1, L0_xattn_Wo1, L0_xattn_bo1, L0_xattn_Wq2, L0_xattn_Wk2, L0_xattn_Wv2, L0_xattn_Wo2, L0_xattn_bo2, L0_xattn_Wp, L0_xattn_bp, L0_xattn_Wf, L0_xattn_bf, L0_xattn_g1, L0_xattn_b1, L0_xattn_g2, L0_xattn_b2, L0_xattn_g3, L0_xattn_b3)
    x = _L1_xattn_ref(x, ctx_768, L1_xattn_Wq, L1_xattn_bq, L1_xattn_Wk, L1_xattn_bk, L1_xattn_Wv, L1_xattn_bv, L1_xattn_Wo, L1_xattn_bo, L1_xattn_ln_g, L1_xattn_ln_b, L1_xattn_W1, L1_xattn_b1, L1_xattn_W2, L1_xattn_b2)
    return x

_drawn_inputs = setup_inputs


def setup_inputs(seed=0):
    import zlib

    import numpy as np

    out = dict(_drawn_inputs(seed))
    spreads = {'L0_xattn_bo1': (0.0, 0.1),
     'L0_xattn_bo2': (0.0, 0.1),
     'L0_xattn_bp': (0.0, 0.1),
     'L0_xattn_bf': (0.0, 0.1),
     'L0_xattn_g1': (1.0, 0.2),
     'L0_xattn_b1': (0.0, 0.1),
     'L0_xattn_g2': (1.0, 0.2),
     'L0_xattn_b2': (0.0, 0.419),
     'L0_xattn_g3': (1.0, 0.2),
     'L0_xattn_b3': (0.0, 0.1),
     'L1_xattn_ln_g': (1.0, 0.2),
     'L1_xattn_ln_b': (0.0, 0.524)}
    factors = {'L1_xattn_bq': 37.478, 'L1_xattn_bk': 64.0, 'L1_xattn_b1': 6.498, 'L1_xattn_b2': 4.643}
    for name, (base, spread) in spreads.items():
        noise = np.random.default_rng([zlib.crc32(name.encode()), seed]).standard_normal(out[name].shape)
        drawn = base * np.exp(spread * noise) if base else spread * noise
        out[name] = jnp.asarray(drawn.astype(out[name].dtype))
    for name, factor in factors.items():
        out[name] = (out[name] * factor).astype(out[name].dtype)
    return out
```

```python
from contextlib import ExitStack

import concourse.bass as bass
from concourse import mybir

F32 = mybir.dt.float32
F32R = mybir.dt.float32r
ALU = mybir.AluOpType
ACT = mybir.ActivationFunctionType
AX = mybir.AxisListType

B, N, D = 16, 112, 256
S, C = 375, 192
H = 16
NP = H // 2
DH = 64
INNER = H * DH
DL = D // H
FF = 4 * D
KT = D // 128
ST = 126
NS = 3
SP = NS * ST
CR = C - 128
GB = 4
NG = B // GB
GT = GB * N
EPS = 1e-5
LAG = 3


def f32(ap):
    return ap.bitcast(F32)


class Core:
    pass


def resident(nc, ctx, k):
    sb = lambda name, shape, dt=F32: ctx.enter_context(nc.sbuf_tensor(name, shape, dt))
    k.x = sb("x_tokens", [N, 1 + B + GB, D])
    k.ident = sb("ident", [128, 128])
    k.stage = sb("w_stage", [128, 3, 2048])
    k.vrows = sb("vector_rows", [NCOL, 128])
    k.consts = sb("vector_columns", [128, NCOL])
    k.bcast = sb("bias_rows", [N, 3, D])
    k.half = sb("minus_half", [N, GB])
    k.eps = sb("eps", [N, GB])
    k.ones = sb("ones", [128, 1])
    k.bank = [ctx.enter_context(nc.psum_tensor(f"bank{i}", [128, 512], F32)) for i in range(8)]
    k.sem = lambda name: ctx.enter_context(nc.semaphore(name))


COLUMNS = {"L0_xattn_g1": 1, "L0_xattn_b1": 3, "L0_xattn_g2": 5, "L0_xattn_b2": 7, "L0_xattn_g3": 9,
           "L0_xattn_b3": 11, "L0_xattn_bp": 13, "L0_xattn_bf": 29, "L1_xattn_ln_g": 31,
           "L1_xattn_ln_b": 33, "L1_xattn_b1": 35, "L1_xattn_b2": 43}
SLOT_COLUMNS = {"L1_xattn_bq": 45, "L1_xattn_bk": 49, "L1_xattn_bv": 53}
NCOL = 57
ROWS = ["L0_xattn_bo1", "L0_xattn_bo2", "L1_xattn_bo"]
WEIGHTS = ["L0_xattn_Wq1", "L0_xattn_Wk1", "L0_xattn_Wv1", "L0_xattn_Wq2", "L0_xattn_Wk2", "L0_xattn_Wv2", "L0_xattn_Wp",
           "L0_xattn_Wf", "L1_xattn_Wq", "L1_xattn_Wk", "L1_xattn_Wv", "L1_xattn_W1", "L1_xattn_W2"]
VECTOR_LOADS = 16 * (len(COLUMNS) + 2 * len(SLOT_COLUMNS))
ROW_LOADS = 16 * len(ROWS)


def phase_semaphores(k, turn):
    def get(name):
        if name not in k.shared[turn]:
            k.shared[turn][name] = k.sem(("even_", "odd_")[turn] + name)
        return k.shared[turn][name]
    return get


def clear_semaphores(sp, k, turn):
    for s in k.shared[turn].values():
        sp.sem_clear(s)


def load_vectors(sp, k, a):
    for name, at in COLUMNS.items():
        n = a[name].shape[0] // 128
        sp.dma_start(k.vrows[at:at + n, :], a[name].rearrange("(c p) -> c p", p=128)).then_inc(k.c_in, 16)
    for name, at in SLOT_COLUMNS.items():
        for twice in range(2):
            sp.dma_start(k.vrows[at:at + 4, :].rearrange("m (s t d) -> m s t d", s=4, t=2)[:, :, twice, :],
                         a[name].rearrange("(m s d) -> m s d", s=4, d=DL)).then_inc(k.c_in, 16)


def load_rows(sp, k, a):
    for i, name in enumerate(ROWS):
        sp.dma_start(k.bcast[:, i, :], a[name].rearrange("(o n) -> o n", o=1).to_broadcast([N, D])
                     ).then_inc(k.rows_in, 16)


class LN:

    def __init__(self, nc, sb, sem, p, src, gain, shift, norm=True):
        self.src, self.gain, self.shift, self.norm = src, gain, shift, norm
        self.st = sb(p + "ln_stats", [N, GB, 6])
        self.mv = sb(p + "ln_mean_var", [N, GB, 2])
        self.ve = sb(p + "ln_var_eps", [N, GB])
        self.rs = sb(p + "ln_rstd", [N, GB])
        self.xh = sb(p + "ln_out", [N, GB, D])
        self.yf = sb(p + "xT", [128, KT, GT])
        self.hi = sb(p + "xT_hi", [128, KT, GT], F32R)
        self.lo = sb(p + "xT_lo", [128, KT, GT], F32R)
        self.stats_done = sem(p + "ln_stats_done")
        self.mean_done = sem(p + "ln_mean_done")
        self.stats_seen = sem(p + "ln_stats_seen")
        self.var_done = sem(p + "ln_var_done")
        self.rstd_done = sem(p + "ln_rstd_done")
        self.norm_done = sem(p + "ln_norm_done")
        self.turned = sem(p + "ln_turned")
        self.full_done = sem(p + "ln_full_done")
        self.hi_done = sem(p + "ln_hi_done")
        self.lo_done = sem(p + "ln_lo_done")

    def dve_stats(self, nc, dve, g, k):
        if not isinstance(g, int):
            dve.wait_ge(self.mean_done, g * GB)
        nc.vector.bn_stats(self.st[:, k, :], self.src[:, bass.ds(g * GB + k + 1, 1), :].rearrange("p a d -> p (a d)")
                           ).then_inc(self.stats_done, 1)

    def dve_mean(self, nc, dve, g, first=False):
        dve.wait_ge(self.stats_done, (g + 1) * GB)
        if not first:
            dve.wait_ge(self.norm_done, g * GB)
            dve.sem_inc(self.stats_seen, 1)
        for k in range(GB):
            nc.vector.bn_aggr(self.mv[:, k, :], self.st[:, k, :]).then_inc(self.mean_done, 1)

    def dve_norm(self, nc, dve, g, k, first=False):
        if not first:
            dve.wait_ge(self.turned, g * GB * KT)
        src = self.src[:, bass.ds(g * GB + k + 1, 1), :].rearrange("p a d -> p (a d)")
        if self.norm:
            dve.wait_ge(self.rstd_done, g + 1)
            nc.vector.tensor_scalar(self.xh[:, k, :], src, self.mv[:, k, 0:1], self.rs[:, k:k + 1],
                                    ALU.subtract, ALU.mult).then_inc(self.norm_done, 1)
        else:
            nc.vector.tensor_copy(self.xh[:, k, :], src).then_inc(self.norm_done, 1)

    def pool_rstd(self, nc, pool, k, g):
        pool.wait_ge(self.mean_done, (g + 1) * GB)
        if not isinstance(g, int):
            pool.wait_ge(self.norm_done, g * GB)
        nc.gpsimd.tensor_tensor(self.ve[:, :], self.mv[:, :, 1], k.eps[:, :], ALU.add).then_inc(self.var_done, 1)
        pool.wait_ge(self.var_done, g + 1)
        nc.gpsimd.tensor_tensor(self.rs[:, :], self.ve[:, :], k.half[:, :], ALU.pow).then_inc(self.rstd_done, 1)

    def pe_turn(self, nc, pe, k, g, banks):
        for b in range(GB):
            pe.wait_ge(self.norm_done, g * GB + b + 1)
            for t in range(KT):
                nc.tensor.transpose(banks[t][:, b * N:(b + 1) * N], self.xh[:, b, t * 128:(t + 1) * 128],
                                    k.ident[0:N, 0:N]).then_inc(self.turned, 1)

    def act_full(self, nc, act, g, banks):
        act.wait_ge(self.turned, (g + 1) * GB * KT)
        if not isinstance(g, int):
            act.wait_ge(self.lo_done, g * KT)
        for t in range(KT):
            if self.norm:
                ins = nc.scalar.activation(self.yf[:, t, :], banks[t][:, 0:GT], ACT.Identity,
                                           bias=self.shift[:, t:t + 1], scale=self.gain[:, t:t + 1])
            else:
                ins = nc.scalar.activation(self.yf[:, t, :], banks[t][:, 0:GT], ACT.Copy)
            ins.then_inc(self.full_done, 1)

    def split(self, eng, k, g):
        for t in range(KT):
            eng.wait_ge(self.full_done, g * KT + t + 1)
            eng.tensor_tensor(self.hi[:, t, :], self.yf[:, t, :], k.ones[:, :].to_broadcast([128, GT]), ALU.mult
                              ).then_inc(self.hi_done, 1)
        for t in range(KT):
            eng.wait_ge(self.hi_done, g * KT + t + 1)
            eng.tensor_tensor(self.lo[:, t, :], self.yf[:, t, :], f32(self.hi[:, t, :]), ALU.subtract
                              ).then_inc(self.lo_done, 1)


def mm3(nc, out, wh, wl, xh, xl, kt, last=True):
    for t in range(kt):
        nc.tensor.matmul(out, wh(t), xh(t), start=(t == 0), stop=False)
        nc.tensor.matmul(out, wh(t), xl(t), start=False, stop=False)
        ins = nc.tensor.matmul(out, wl(t), xh(t), start=False, stop=(t == kt - 1))
    return ins


def self_attention(nc, k, a, nxt):
    with ExitStack() as ctx:
        sb = lambda name, shape, dt=F32: ctx.enter_context(nc.sbuf_tensor("A_" + name, shape, dt))
        sem = phase_semaphores(k, 0)
        wh = [sb(f"w{w}_hi", [128, KT, INNER], F32R) for w in "qkv"]
        wl = [sb(f"w{w}_lo", [128, KT, INNER], F32R) for w in "qkv"]
        wo = sb("wo", [128, NP, D])
        ln = LN(nc, sb, sem, "", k.x, k.consts[:, 1:3], k.consts[:, 3:5])
        q = sb("q", [128, NP, GT])
        kb = sb("k_blocks", [128, NP, GB, 2, N])
        v = sb("v", [N, GB, INNER])
        P = sb("probs", [N, 4, 2, N])
        PT = sb("probsT", [N, 4, 2, N])
        oT = sb("oT", [128, NP, N])
        nm = sb("neg_max", [N, 4, 2])
        sm = sb("sums", [N, 4, 2])
        rc = sb("rsums", [N, 4, 2])
        tmp = sb("attn_out", [N, D])
        SB, TB, OB = k.bank[0:2], k.bank[2:4], k.bank[4:6]
        PJ = k.bank[6:8]

        wo_in, w_hi, w_lo = sem("wo_in"), sem("w_hi"), sem("w_lo")
        init = sem("init")
        pj_done, pj_act, pj_dve = sem("proj_done"), sem("proj_out_act"), sem("proj_out_dve")
        s_done, max_done, exp_done = sem("scores_done"), sem("max_done"), sem("exp_done")
        rcp_done, norm_done, t_done = sem("rcp_done"), sem("norm_done"), sem("turned")
        pt_out, av_done, o_out = sem("probsT_out"), sem("av_done"), sem("oT_out")
        y_done, y_out, x_done = sem("y_done"), sem("y_out"), sem("x_done")
        SEQ0 = NP
        EXP0, NORM0, T0, PT0, AV0, O0, Y0 = 2 * 2, SEQ0, 4 + NP - LAG, 2 + NP - LAG, 4 + NP - LAG - 1, 2 + 1, 1
        QK, V = 2 * NP, 2 * GB
        UNITS = QK + V

        block = ctx.enter_context(nc.Block(no_gpsimd_drain=True))

        @block.sync
        def _(sp):
            xs = a["x"].rearrange("b n d -> n b d")
            sp.dma_start(k.x[:, 1:1 + GB, :], xs[:, 0:GB, :]).then_inc(k.x_in[0], 16)
            load_vectors(sp, k, a)
            for w, name in enumerate(("L0_xattn_Wq1", "L0_xattn_Wk1", "L0_xattn_Wv1")):
                sp.dma_start(k.stage[:, w, :].rearrange("p (t n) -> p t n", t=KT),
                             a[name].rearrange("(t p) n -> p t n", p=128)).then_inc(k.w_in[name], 16)
            sp.dma_start(k.x[:, 1 + GB:1 + B, :], xs[:, GB:B, :]).then_inc(k.x_in[1], 16)
            load_rows(sp, k, a)
            sp.dma_start(wo[:, :, :], a["L0_xattn_Wo1"].rearrange("(t p) n -> p t n", p=128)).then_inc(wo_in, 16)
            sp.wait_ge(w_hi, 3)
            sp.wait_ge(w_lo, 3)
            nxt(sp)
            sp.wait_ge(ln.lo_done, (NG + 1) * KT)

        @block.gpsimd
        def _(pool):
            nc.gpsimd.memset(k.half[:, :], -0.5).then_inc(k.half_set, 1)
            nc.gpsimd.memset(k.eps[:, :], EPS).then_inc(k.half_set, 1)
            nc.gpsimd.memset(k.ones[:, :], 1.0).then_inc(k.half_set, 1)
            nc.gpsimd.memset(k.ident[:, :], 0.0).then_inc(k.ident_set, 1)
            pool.wait_ge(k.ident_set, 1)
            nc.gpsimd.affine_select(out=k.ident[:, :], in_=k.ident[:, :], compare_op=ALU.not_equal, fill=1.0, base=0,
                                    pattern=[[-1, 128]], channel_multiplier=1).then_inc(k.ident_set, 1)
            mask = k.vrows[0:1, :].rearrange("p (s t d) -> p s t d", s=4, t=2)
            for half in range(2):
                nc.gpsimd.memset(mask[:, :, half, :], -float(half)).then_inc(k.mask_set, 1)
            pool.wait_ge(k.half_set, 3)
            ln.pool_rstd(nc, pool, k, 0)
            nc.gpsimd.memset(k.x[:, 1 + B:1 + B + GB, :], 0.0).then_inc(k.pad_set, 1)
            nc.gpsimd.memset(k.x[:, 0, :], 0.0).then_inc(k.pad_set, 1)
            nc.gpsimd.memset(P[:, :, :, :], 0.0).then_inc(init, 1)
            nc.gpsimd.memset(PT[:, :, :, :], 0.0).then_inc(init, 1)
            nc.gpsimd.memset(v[:, GB - 1, :], 0.0).then_inc(init, 1)
            nc.gpsimd.memset(oT[:, :, :], 0.0).then_inc(init, 1)
            with pool.Fori(0, NG) as g:
                ln.pool_rstd(nc, pool, k, g + 1)
                ln.split(nc.gpsimd, k, g + 1)

        @block.scalar
        def _(act):
            for w in range(3):
                act.wait_ge(k.w_in[f"L0_xattn_W{'qkv'[w]}1"], 16)
                nc.scalar.activation(wh[w][:, :, :].rearrange("p t n -> p (t n)"), k.stage[:, w, :], ACT.Copy
                                     ).then_inc(w_hi, 1)
                if w == 0:
                    act.wait_ge(k.cols_turned, 1)
                    nc.scalar.activation(k.consts[:, :], k.bank[0][:, 0:NCOL], ACT.Copy).then_inc(k.cols_set, 1)
                    act.wait_ge(k.cols_set, 1)
                    ln.act_full(nc, act, 0, PJ)
            act.sem_inc(exp_done, EXP0)
            act.sem_inc(o_out, O0)
            act.sem_inc(pt_out, PT0)

            def exps(t, u):
                act.wait_ge(max_done, t * NP + u + 1)
                act.wait_ge(t_done, (t + 1) * NP + u + 1)
                for j in range(2):
                    nc.scalar.activation(P[:, u % 4, j, :], SB[u % 2][0:N, j * N:(j + 1) * N], ACT.Exp,
                                         bias=nm[:, u % 4, j:j + 1],
                                         accum_out=sm[:, u % 4, j:j + 1]).then_inc(exp_done, 1)

            def pt_evac(t, u):
                act.wait_ge(t_done, 4 + (t + 1) * NP + u + 1)
                act.wait_ge(av_done, (t + 1) * NP + u + 1)
                nc.scalar.activation(PT[:, u % 4, :, :].rearrange("p j n -> p (j n)"), TB[u % 2][0:N, 0:2 * N],
                                     ACT.Copy).then_inc(pt_out, 1)

            def o_evac(t, h):
                act.wait_ge(av_done, 4 + (t + 1) * NP + 4 * h + 4)
                act.wait_ge(y_done, t + 1)
                nc.scalar.activation(oT[:, 4 * h:4 * h + 4, :].rearrange("p u n -> p (u n)"),
                                     OB[h][:, 0:4 * N], ACT.Copy).then_inc(o_out, 1)

            def late(t, i):
                if i < LAG:
                    pt_evac(t, NP - LAG + i)
                if i == LAG:
                    o_evac(t, 1)

            with act.Fori(0, NG) as g:
                for i in range(UNITS // 2):
                    act.wait_ge(pj_done, g * UNITS + 2 * i + 1)
                    if i < NP:
                        ins = nc.scalar.activation(q[:, i, :], PJ[0][:, 0:GT], ACT.Copy, scale=DH ** -0.5)
                    else:
                        ins = nc.scalar.activation(v[:, i - NP, 0:512], PJ[0][0:N, :], ACT.Copy)
                    ins.then_inc(pj_act, 1)
                    late(g * GB - 1, i)
                ln.act_full(nc, act, g + 1, PJ)
                for b in range(GB):
                    t = g * GB + b
                    for u in range(NP):
                        exps(t, u)
                        if u >= LAG:
                            pt_evac(t, u - LAG)
                        if b > 0:
                            late(t - 1, u)
                        if u == NP - 1:
                            o_evac(t, 0)
            for i in range(LAG + 1):
                late(B - 1, i)

        @block.vector
        def _(dve):
            dve.sem_inc(y_out, Y0)
            dve.sem_inc(norm_done, NORM0)
            nc.vector.memset(kb[:, :, :, :, :].rearrange("p u b j n -> p (u b j n)"), 0.0).then_inc(init, 1)
            dve.wait_ge(k.x_in[0], 16)
            for b in range(GB):
                ln.dve_stats(nc, dve, 0, b)
            ln.dve_mean(nc, dve, 0, True)
            for b in range(GB):
                ln.dve_norm(nc, dve, 0, b, True)
            for w in range(3):
                dve.wait_ge(w_hi, w + 1)
                nc.vector.tensor_tensor(wl[w][:, :, :].rearrange("p t n -> p (t n)"), k.stage[:, w, :],
                                        f32(wh[w][:, :, :]).rearrange("p t n -> p (t n)"), ALU.subtract
                                        ).then_inc(w_lo, 1)
                if w == 0:
                    ln.split(nc.vector, k, 0)
            dve.wait_ge(init, 5)
            dve.wait_ge(k.x_in[1], 16)
            dve.wait_ge(k.pad_set, 2)
            dve.wait_ge(k.rows_in, ROW_LOADS)

            def maxima(t, u):
                dve.wait_ge(s_done, t * NP + u + 1)
                nc.vector.tensor_reduce(nm[:, u % 4, :], SB[u % 2][0:N, 0:2 * N].rearrange("p (j n) -> p j n", j=2),
                                        AX.X, ALU.max, negate=True).then_inc(max_done, 1)

            def norm(t, u):
                dve.wait_ge(exp_done, EXP0 + t * 2 * NP + 2 * u + 2)
                nc.vector.reciprocal(rc[:, u % 4, :], sm[:, u % 4, :]).then_inc(rcp_done, 1)
                dve.wait_ge(rcp_done, t * NP + u + 1)
                nc.vector.tensor_tensor(P[:, u % 4, :, :], P[:, u % 4, :, :],
                                        rc[:, u % 4, :].unsqueeze(2).to_broadcast([N, 2, N]),
                                        ALU.mult).then_inc(norm_done, 1)

            def x_update(t, bank):
                dve.wait_ge(y_done, t + 2)
                dve.wait_ge(x_done, t + 1)
                nc.vector.tensor_tensor(tmp[:, :], bank[0:N, 0:D], k.bcast[:, 0, :], ALU.add).then_inc(y_out, 1)
                dve.wait_ge(y_out, Y0 + t + 2)
                xt = k.x[:, bass.ds(t + 1, 1), :].rearrange("p a d -> p (a d)")
                nc.vector.tensor_tensor(xt, xt, tmp[:, :], ALU.add).then_inc(x_done, 1)

            with dve.Fori(0, NG) as g:
                for i in range(UNITS // 2):
                    dve.wait_ge(pj_done, g * UNITS + 2 * i + 2)
                    if i < NP:
                        for j in range(2):
                            r = slice(64 * j, 64 * j + 64)
                            ins = nc.vector.tensor_copy(
                                kb[r, i, :, j, :], PJ[1][r, 0:GT].rearrange("p (b n) -> p b n", b=GB))
                            ins.then_inc(pj_dve, 1)
                    else:
                        nc.vector.tensor_copy(v[:, i - NP, 512:1024], PJ[1][0:N, :]).then_inc(pj_dve, 1)
                    if i < GB:
                        ln.dve_stats(nc, dve, g + 1, i)
                    if i == GB:
                        ln.dve_mean(nc, dve, g + 1)
                    if i == 6:
                        x_update(g * GB - 1, SB[0])
                    if i >= 8:
                        ln.dve_norm(nc, dve, g + 1, i - 8)
                for b in range(GB):
                    t = g * GB + b
                    for u in range(NP):
                        maxima(t, u)
                        if u > 0:
                            norm(t, u - 1)
                    norm(t, NP - 1)
                    if b > 0:
                        x_update(t - 1, PJ[0])
            x_update(B - 1, SB[0])

        @block.tensor
        def _(pe):
            pe.wait_ge(k.ident_set, 2)
            pe.wait_ge(k.c_in, VECTOR_LOADS)
            pe.wait_ge(k.mask_set, 2)
            nc.tensor.transpose(k.bank[0][:, 0:NCOL], k.vrows[:, :], k.ident[0:NCOL, 0:NCOL]).then_inc(k.cols_turned, 1)
            ln.pe_turn(nc, pe, k, 0, PJ)
            pe.wait_ge(k.cols_set, 1)
            pe.sem_inc(t_done, T0)
            pe.sem_inc(av_done, AV0)
            pe.wait_ge(w_lo, 1)
            pe.wait_ge(init, 5)
            pe.wait_ge(wo_in, 16)

            def scores(b, t, u):
                pe.wait_ge(exp_done, t * 2 * NP + 2 * u + 2)
                nc.tensor.matmul(SB[u % 2][0:N, 0:2 * N], q[:, u, b * N:(b + 1) * N],
                                 kb[:, u, b, :, :].rearrange("p j n -> p (j n)"),
                                 start=True, stop=True).then_inc(s_done, 1)

            def turn(t, u):
                pe.wait_ge(norm_done, (t + 1) * NP + u + 1)
                pe.wait_ge(pt_out, (t + 1) * NP + u + 1)
                for j in range(2):
                    ins = nc.tensor.transpose(TB[u % 2][0:N, j * N:(j + 1) * N], P[:, u % 4, j, :], k.ident[0:N, 0:N])
                ins.then_inc(t_done, 1)

            def values(b, t, u):
                pe.wait_ge(pt_out, 2 + (t + 1) * NP + u + 1)
                if u % 4 == 0:
                    pe.wait_ge(o_out, (t + 1) * 2 + u // 4 + 1)
                for j in range(2):
                    h = 2 * u + j
                    ins = nc.tensor.matmul(OB[u // 4][64 * j:64 * j + 64, (u % 4) * N:(u % 4 + 1) * N],
                                           v[:, b, h * DH:(h + 1) * DH], PT[:, u % 4, j, :], start=True, stop=True)
                ins.then_inc(av_done, 1)

            def project(t, bank, part, parts):
                if part == 0:
                    pe.wait_ge(o_out, 2 + 2 * (t + 2))
                    pe.wait_ge(y_out, t + 2)
                n = NP // parts
                for u in range(part * n, part * n + n):
                    ins = nc.tensor.matmul(bank[0:N, 0:D], oT[:, u, :], wo[:, u, :], start=(u == 0), stop=(u == NP - 1))
                if part == parts - 1:
                    ins.then_inc(y_done, 1)

            def late(b, t, i, bank, parts):
                if i < LAG:
                    turn(t, NP - LAG + i)
                if i <= LAG:
                    values(b, t, NP - LAG - 1 + i)
                if LAG < i <= LAG + parts:
                    project(t, bank, i - LAG - 1, parts)

            with pe.Fori(0, NG) as g:
                pe.wait_ge(ln.lo_done, (g + 1) * KT)
                pe.wait_ge(y_out, g * GB + Y0)
                for i in range(UNITS):
                    if i >= 2 and i % 2 == 0:
                        pe.wait_ge(pj_act, g * (UNITS // 2) + i // 2)
                    if i >= 2 and i % 2 == 1:
                        pe.wait_ge(pj_dve, g * (2 * NP + GB) + min(i // 2, NP) * 2 + max(i // 2 - NP, 0))
                    if i == 1:
                        pe.wait_ge(w_lo, 2)
                    if i < QK:
                        w, m = i % 2, slice(128 * (i // 2), 128 * (i // 2 + 1))
                        ins = mm3(nc, PJ[i % 2][:, 0:GT], lambda t: wh[w][:, t, m], lambda t: wl[w][:, t, m],
                                  lambda t: ln.hi[:, t, :], lambda t: ln.lo[:, t, :], KT)
                    else:
                        if i == QK:
                            pe.wait_ge(w_lo, 3)
                        b, n = (i - QK) // 2, slice(512 * (i % 2), 512 * (i % 2 + 1))
                        tok = slice(b * N, (b + 1) * N)
                        ins = mm3(nc, PJ[i % 2][0:N, :], lambda t: ln.hi[:, t, tok], lambda t: ln.lo[:, t, tok],
                                  lambda t: wh[2][:, t, n], lambda t: wl[2][:, t, n], KT)
                    ins.then_inc(pj_done, 1)
                    if i % 2 == 1:
                        late(GB - 1, g * GB - 1, i // 2, SB[0], 1)
                pe.wait_ge(pj_act, (g + 1) * (UNITS // 2))
                pe.wait_ge(pj_dve, (g + 1) * (2 * NP + GB))
                ln.pe_turn(nc, pe, k, g + 1, PJ)
                pe.wait_ge(y_out, g * GB + Y0 + 1)
                for b in range(GB):
                    t = g * GB + b
                    for u in range(NP):
                        scores(b, t, u)
                        if b > 0:
                            if u == LAG + 1:
                                pe.wait_ge(ln.full_done, (g + 2) * KT)
                            late(b - 1, t - 1, u, PJ[0], 4)
                        if u >= LAG:
                            turn(t, u - LAG)
                        if u > LAG:
                            values(b, t, u - LAG - 1)
            for i in range(LAG + 2):
                late(GB - 1, B - 1, i, SB[0], 1)


def context_weights_in(sp, stage, w, sem):
    n = w.shape[1]
    at = stage[:, 0:2 * n].rearrange("p (t n) -> p t n", t=2)
    sp.dma_start(at[:, 0, :], w[0:128, :]).then_inc(sem, 16)
    sp.dma_start(at[0:CR, 1, :], w[128:C, :]).then_inc(sem, 16)
    sp.dma_start(at[CR:128, 1, :], w[128:C, :]).then_inc(sem, 16)


CONTEXT_LOADS = 3 * 16


def mm5(nc, out, lh, rh, turned):
    (w, wl), (c0, c0l, c1) = (rh, lh) if turned else (lh, rh)
    passes = [(w[0], c0), (w[0], c0l), (wl[0], c0), (w[1], c1), (wl[1], c1)]
    for i, (x, y) in enumerate(passes):
        ins = nc.tensor.matmul(out, y if turned else x, x if turned else y, start=(i == 0), stop=(i == 4))
    return ins


class Context:

    def __init__(self, nc, sb, sem):
        self.raw = sb("ctx", [ST, NS, C])
        self.T = sb("ctxT", [128, 3, SP], F32R)
        self.cleared = sem("ctx_cleared")
        self.loaded = sem("ctx_loaded")
        self.turned = sem("ctx_turned")
        self.hi_done = sem("ctx_hi_done")
        self.lo_done = sem("ctx_lo_done")

    LOADS = 32

    def load(self, sp, c, t):
        src = c[bass.ds(t, 1), :, :].rearrange("a s c -> (a s) c")
        sp.dma_start(self.raw[:, 0:NS - 1, :], src[0:ST * (NS - 1), :].rearrange("(n p) c -> p n c", p=ST)
                     ).then_inc(self.loaded, 16)
        sp.dma_start(self.raw[0:S - ST * (NS - 1), NS - 1, :], src[ST * (NS - 1):S, :]).then_inc(self.loaded, 16)

    def sp_loop(self, sp, c):
        with sp.Fori(1, B) as t:
            sp.wait_ge(self.turned, t)
            self.load(sp, c, t)
        sp.wait_ge(self.turned, B)
        self.load(sp, c, 0)
        sp.wait_ge(self.turned, B + 1)

    def pe_turn(self, nc, pe, k, t, banks):
        pe.wait_ge(self.loaded, (t + 1) * self.LOADS)
        for s in range(NS):
            cols = slice(ST * s, ST * (s + 1))
            nc.tensor.transpose(banks[0][:, cols], self.raw[:, s, 0:128], k.ident[0:ST, 0:ST])
            ins = nc.tensor.transpose(banks[1][0:CR, cols], self.raw[:, s, 128:C], k.ident[0:ST, 0:ST])
        ins.then_inc(self.turned, 1)

    def act_hi(self, nc, act, t, banks):
        act.wait_ge(self.turned, t + 1)
        nc.scalar.activation(self.T[:, 0, :], banks[0][:, 0:SP], ACT.Copy).then_inc(self.hi_done, 1)
        nc.scalar.activation(self.T[0:CR, 2, :], banks[1][0:CR, 0:SP], ACT.Copy).then_inc(self.hi_done, 1)

    def dve_lo(self, nc, dve, t, banks):
        dve.wait_ge(self.hi_done, 2 * (t + 1))
        nc.vector.tensor_tensor(self.T[:, 1, :], banks[0][:, 0:SP], f32(self.T[:, 0, :]), ALU.subtract
                                ).then_inc(self.lo_done, 1)
        nc.vector.tensor_tensor(self.T[CR:128, 2, :], banks[1][0:CR, 0:SP], f32(self.T[0:CR, 2, :]), ALU.subtract
                                ).then_inc(self.lo_done, 1)

    def cols(self, at):
        return [self.T[:, i, at] for i in range(3)]


def cross_attention(nc, k, a, nxt):
    with ExitStack() as ctx:
        sb = lambda name, shape, dt=F32: ctx.enter_context(nc.sbuf_tensor("B_" + name, shape, dt))
        sem = phase_semaphores(k, 1)
        LAG = 2
        wqh, wkh, wvh = [sb(f"w{w}_hi", [128, 2, INNER], F32R) for w in "qkv"]
        wql, wkl, wvl = [sb(f"w{w}_lo", [128, 2, INNER], F32R) for w in "qkv"]
        wo = sb("wo", [128, NP, D])
        ln = LN(nc, sb, sem, "", k.x, k.consts[:, 5:7], k.consts[:, 7:9])
        cx = Context(nc, sb, sem)
        qg = sb("q_group", [128, NP, GT])
        qh = sb("q_hi", [128, NP, N], F32R)
        ql = sb("q_lo", [128, NP, N], F32R)
        kh = sb("k_hi", [128, NP, SP], F32R)
        kl = sb("k_lo", [128, NP, SP], F32R)
        v = sb("v", [ST, NS, INNER])
        P = sb("probs", [N, 2, 2, SP])
        PT = sb("probsT", [ST, 2, 2, NS, N])
        oT = sb("oT", [128, NP, N])
        nm = sb("neg_max", [N, 2, 2])
        sm = sb("sums", [N, 2, 2])
        rc = sb("rsums", [N, 2, 2])
        tmp = sb("attn_out", [N, D])
        SB, TB, OB, YB, PJ = k.bank[0:2], k.bank[2:4], k.bank[4], k.bank[5], k.bank[6:8]

        wo_in, w_hi, w_lo, init = sem("wo_in"), sem("w_hi"), sem("w_lo"), sem("init")
        q_mm, q_act, q_dve, qh_done, ql_done = sem("q_mm"), sem("q_act"), sem("q_dve"), sem("qh"), sem("ql")
        k_mm, k_hi, k_lo = sem("k_mm"), sem("k_hi_done"), sem("k_lo_done")
        v_mm, v_out = sem("v_mm"), sem("v_out")
        s_done, max_done, exp_done = sem("scores_done"), sem("max_done"), sem("exp_done")
        rcp_done, norm_done, t_done = sem("rcp_done"), sem("norm_done"), sem("turned")
        pt_act, pt_dve, av_done, o_out = sem("probsT_act"), sem("probsT_dve"), sem("av_done"), sem("oT_out")
        y_done, y_out, x_done = sem("y_done"), sem("y_out"), sem("x_done")
        EXP0, NORM0, T0, PT0, AV0, O0, Y0 = 2, NP, 2 + NP - LAG, 1 + NP - LAG, 2 + NP - LAG - 1, 1 + 1, 1

        block = ctx.enter_context(nc.Block(no_gpsimd_drain=True))

        @block.sync
        def _(sp):
            sp.dma_start(wo[:, :, :], a["L0_xattn_Wo2"].rearrange("(t p) n -> p t n", p=128)).then_inc(wo_in, 16)
            sp.wait_ge(cx.cleared, 1)
            cx.load(sp, a["ctx_768"], 0)
            sp.wait_ge(w_hi, 3)
            sp.wait_ge(w_lo, 3)
            nxt(sp)
            clear_semaphores(sp, k, 0)
            cx.sp_loop(sp, a["ctx_768"])
            sp.wait_ge(ln.lo_done, (NG + 1) * KT)

        @block.gpsimd
        def _(pool):
            nc.gpsimd.memset(cx.raw[:, :, :], 0.0).then_inc(cx.cleared, 1)
            ln.pool_rstd(nc, pool, k, 0)
            nc.gpsimd.memset(P[:, :, :, :], 0.0).then_inc(init, 1)
            nc.gpsimd.memset(PT[:, :, :, :, :].rearrange("p r j s n -> p (r j s n)"), 0.0).then_inc(init, 1)
            nc.gpsimd.memset(oT[:, :, :], 0.0).then_inc(init, 1)
            with pool.Fori(0, NG) as g:
                ln.pool_rstd(nc, pool, k, g + 1)
                for b in range(GB):
                    t = g * GB + b
                    pool.wait_ge(q_act, (g + 1) * (NP // 2))
                    pool.wait_ge(q_dve, (g + 1) * (NP // 2))
                    for u in range(NP):
                        pool.wait_ge(s_done, 2 * (t * NP + u + 1))
                        nc.gpsimd.tensor_tensor(qh[:, u, :], qg[:, u, b * N:(b + 1) * N],
                                                k.ones[:, :].to_broadcast([128, N]), ALU.mult
                                                ).then_inc(qh_done, 1)
                        pool.wait_ge(qh_done, t * NP + u + 1)
                        nc.gpsimd.tensor_tensor(ql[:, u, :], qg[:, u, b * N:(b + 1) * N], f32(qh[:, u, :]),
                                                ALU.subtract).then_inc(ql_done, 1)
                ln.split(nc.gpsimd, k, g + 1)

        @block.scalar
        def _(act):
            for i, (w, src) in enumerate(((wkh, 1), (wqh, 0), (wvh, 2))):
                act.wait_ge(k.w_in[f"L0_xattn_W{'qkv'[src]}2"], 16 if src == 0 else CONTEXT_LOADS)
                nc.scalar.activation(w[:, :, :].rearrange("p t n -> p (t n)"), k.stage[:, src, :], ACT.Copy
                                     ).then_inc(w_hi, 1)
                if i == 0:
                    cx.act_hi(nc, act, 0, k.bank[2:4])
                    ln.act_full(nc, act, 0, PJ)
            act.sem_inc(o_out, O0)
            act.sem_inc(exp_done, EXP0)
            act.sem_inc(pt_act, PT0)

            def exps(t, u):
                act.wait_ge(t_done, (t + 1) * NP + u + 1)
                for j in range(2):
                    act.wait_ge(max_done, 2 * (t * NP + u) + j + 1)
                    nc.scalar.activation(P[:, u % 2, j, 0:S], SB[j][0:N, 0:S], ACT.Exp, bias=nm[:, u % 2, j:j + 1],
                                         accum_out=sm[:, u % 2, j:j + 1]).then_inc(exp_done, 1)

            def pt_evac(t, u):
                act.wait_ge(t_done, 2 + (t + 1) * NP + u + 1)
                act.wait_ge(av_done, (t + 1) * NP + u + 1)
                nc.scalar.activation(PT[:, u % 2, 0, :, :].rearrange("p s n -> p (s n)"), TB[0][0:ST, 0:NS * N],
                                     ACT.Copy).then_inc(pt_act, 1)

            def o_evac(t, h):
                act.wait_ge(av_done, 2 + (t + 1) * NP + 4 * h + 4)
                act.wait_ge(y_done, t + 1)
                nc.scalar.activation(oT[:, 4 * h:4 * h + 4, :].rearrange("p u n -> p (u n)"),
                                     OB[:, 0:4 * N], ACT.Copy).then_inc(o_out, 1)

            def keys(t, u, bank):
                act.wait_ge(k_mm, t * NP + u + 1)
                nc.scalar.activation(kh[:, u, :], bank[:, 0:SP], ACT.Copy).then_inc(k_hi, 1)

            for u in range(2):
                keys(0, u, PJ[u])
            with act.Fori(0, NG) as g:
                for i in range(NP // 2):
                    act.wait_ge(q_mm, g * NP + 2 * i + 1)
                    act.wait_ge(ql_done, g * GB * NP)
                    nc.scalar.activation(qg[:, 2 * i, :], PJ[0][:, 0:GT], ACT.Copy, scale=DH ** -0.5
                                         ).then_inc(q_act, 1)
                ln.act_full(nc, act, g + 1, PJ)
                with act.Fori(0, GB) as b:
                    t = g * GB + b
                    for u in range(NP):
                        pt_evac(t if u >= LAG else t - 1, (u - LAG) % NP)
                        if u == 2:
                            o_evac(t - 1, 1)
                        if u == NP - 2:
                            o_evac(t, 0)
                            cx.act_hi(nc, act, t + 1, PJ)
                        exps(t, u)
                        if u < NP - 2:
                            keys(t, u + 2, PJ[0])
                            act.wait_ge(v_mm, t * 2 * NS + u + 1)
                            h = u // NS
                            nc.scalar.activation(v[:, u % NS, 512 * h:512 * (h + 1)], PJ[1][0:ST, :], ACT.Copy
                                                 ).then_inc(v_out, 1)
                        if u == NP - 1:
                            for w in range(2):
                                keys(t + 1, w, PJ[w])
            for u in range(NP - LAG, NP):
                pt_evac(B - 1, u)
            o_evac(B - 1, 1)

        @block.vector
        def _(dve):
            dve.sem_inc(y_out, Y0)
            dve.sem_inc(norm_done, NORM0)
            dve.sem_inc(pt_dve, PT0)
            for b in range(GB):
                ln.dve_stats(nc, dve, 0, b)
            ln.dve_mean(nc, dve, 0, True)
            for w in (wkl, wvl):
                nc.vector.memset(f32(w[CR:128, 1, :]), 0.0).then_inc(init, 1)
            nc.vector.memset(v[:, :, :], 0.0).then_inc(init, 1)
            nc.vector.memset(OB[:, 0:4 * N], 0.0).then_inc(init, 1)
            for b in range(GB):
                ln.dve_norm(nc, dve, 0, b, True)
            for i, (w, wh, src) in enumerate(((wkl, wkh, 1), (wql, wqh, 0), (wvl, wvh, 2))):
                dve.wait_ge(w_hi, i + 1)
                if src == 0:
                    nc.vector.tensor_tensor(w[:, :, :].rearrange("p t n -> p (t n)"), k.stage[:, src, :],
                                            f32(wh[:, :, :]).rearrange("p t n -> p (t n)"), ALU.subtract
                                            ).then_inc(w_lo, 1)
                    continue
                raw = k.stage[:, src, :].rearrange("p (t n) -> p t n", t=2)
                nc.vector.tensor_tensor(w[:, 0, :], raw[:, 0, :], f32(wh[:, 0, :]), ALU.subtract)
                nc.vector.tensor_tensor(w[0:CR, 1, :], raw[0:CR, 1, :], f32(wh[0:CR, 1, :]), ALU.subtract
                                        ).then_inc(w_lo, 1)
                if i == 0:
                    cx.dve_lo(nc, dve, 0, k.bank[2:4])
                    ln.split(nc.vector, k, 0)
            dve.wait_ge(init, 7)

            def maxima(t, u):
                for j in range(2):
                    dve.wait_ge(s_done, 2 * (NP + t * NP + u) + j + 1)
                    nc.vector.tensor_reduce(nm[:, u % 2, j:j + 1], SB[j][0:N, 0:S], AX.X, ALU.max, negate=True
                                            ).then_inc(max_done, 1)

            def norm(t, u):
                dve.wait_ge(exp_done, EXP0 + t * 2 * NP + 2 * u + 2)
                nc.vector.reciprocal(rc[:, u % 2, :], sm[:, u % 2, :]).then_inc(rcp_done, 1)
                dve.wait_ge(rcp_done, t * NP + u + 1)
                nc.vector.tensor_tensor(P[:, u % 2, :, 0:S], P[:, u % 2, :, 0:S],
                                        rc[:, u % 2, :].unsqueeze(2).to_broadcast([N, 2, S]),
                                        ALU.mult).then_inc(norm_done, 1)

            def pt_evac(t, u):
                dve.wait_ge(t_done, 2 + (t + 1) * NP + u + 1)
                dve.wait_ge(av_done, (t + 1) * NP + u + 1)
                nc.vector.tensor_copy(PT[:, u % 2, 1, :, :].rearrange("p s n -> p (s n)"), TB[1][0:ST, 0:NS * N]
                                      ).then_inc(pt_dve, 1)

            def keys(t, u, bank):
                dve.wait_ge(k_hi, t * NP + u + 1)
                nc.vector.tensor_tensor(kl[:, u, :], bank[:, 0:SP], f32(kh[:, u, :]), ALU.subtract).then_inc(k_lo, 1)

            def x_update(t):
                dve.wait_ge(y_done, t + 2)
                dve.wait_ge(x_done, t + 1)
                nc.vector.tensor_tensor(tmp[:, :], YB[0:N, 0:D], k.bcast[:, 1, :], ALU.add).then_inc(y_out, 1)
                dve.wait_ge(y_out, Y0 + t + 2)
                xt = k.x[:, bass.ds(t + 1, 1), :].rearrange("p a d -> p (a d)")
                nc.vector.tensor_tensor(xt, xt, tmp[:, :], ALU.add).then_inc(x_done, 1)

            for u in range(2):
                keys(0, u, PJ[u])
            with dve.Fori(0, NG) as g:
                for b in range(GB):
                    ln.dve_stats(nc, dve, g + 1, b)
                ln.dve_mean(nc, dve, g + 1)
                for i in range(NP // 2):
                    dve.wait_ge(q_mm, g * NP + 2 * i + 2)
                    dve.wait_ge(ql_done, g * GB * NP)
                    nc.vector.tensor_scalar(qg[:, 2 * i + 1, :], PJ[1][:, 0:GT], DH ** -0.5, None, ALU.mult
                                            ).then_inc(q_dve, 1)
                    ln.dve_norm(nc, dve, g + 1, i)
                with dve.Fori(0, GB) as b:
                    t = g * GB + b
                    for u in range(NP):
                        if u > 0:
                            norm(t, u - 1)
                        pt_evac(t if u >= LAG else t - 1, (u - LAG) % NP)
                        maxima(t, u)
                        if u < NP - 2:
                            keys(t, u + 2, PJ[0])
                        if u == NP - 2:
                            cx.dve_lo(nc, dve, t + 1, PJ)
                        if u == NP - 1:
                            for w in range(2):
                                keys(t + 1, w, PJ[w])
                    norm(t, NP - 1)
                    x_update(t - 1)
            for u in range(NP - LAG, NP):
                pt_evac(B - 1, u)
            x_update(B - 1)

        @block.tensor
        def _(pe):
            cx.pe_turn(nc, pe, k, 0, k.bank[2:4])
            ln.pe_turn(nc, pe, k, 0, PJ)
            pe.sem_inc(t_done, T0)
            pe.sem_inc(av_done, AV0)
            pe.sem_inc(s_done, 2 * NP)
            pe.wait_ge(w_lo, 1)
            pe.wait_ge(cx.lo_done, 2)

            def keys(t, u, bank):
                m = slice(128 * u, 128 * (u + 1))
                mm5(nc, bank[:, 0:SP], ([wkh[:, i, m] for i in range(2)], [wkl[:, i, m] for i in range(2)]),
                    cx.cols(slice(0, SP)), False).then_inc(k_mm, 1)

            def new_values(t, u):
                h, s = u // NS, u % NS
                n = slice(512 * h, 512 * (h + 1))
                mm5(nc, PJ[1][0:ST, :], cx.cols(slice(ST * s, ST * (s + 1))),
                    ([wvh[:, i, n] for i in range(2)], [wvl[:, i, n] for i in range(2)]), True).then_inc(v_mm, 1)

            def scores(t, u):
                pe.wait_ge(ql_done, t * NP + u + 1)
                pe.wait_ge(k_lo, t * NP + u + 1)
                for i, (x, y) in enumerate(((qh, kh), (qh, kl), (ql, kh))):
                    for j in range(2):
                        if i == 0:
                            pe.wait_ge(exp_done, 2 * (t * NP + u) + j + 1)
                        r = slice(64 * j, 64 * j + 64)
                        ins = nc.tensor.matmul(SB[j][0:N, 0:SP], x[r, u, :], y[r, u, :], start=(i == 0), stop=(i == 2))
                        if i == 2:
                            ins.then_inc(s_done, 1)

            def turn(t, u):
                pe.wait_ge(norm_done, (t + 1) * NP + u + 1)
                pe.wait_ge(pt_act, (t + 1) * NP + u + 1)
                pe.wait_ge(pt_dve, (t + 1) * NP + u + 1)
                for j in range(2):
                    for s in range(NS):
                        ins = nc.tensor.transpose(TB[j][0:ST, s * N:(s + 1) * N],
                                                  P[:, u % 2, j, ST * s:ST * (s + 1)], k.ident[0:N, 0:N])
                ins.then_inc(t_done, 1)

            def values(t, u):
                pe.wait_ge(pt_act, 1 + (t + 1) * NP + u + 1)
                pe.wait_ge(pt_dve, 1 + (t + 1) * NP + u + 1)
                if u % 4 == 0:
                    pe.wait_ge(o_out, (t + 1) * 2 + u // 4 + 1)
                    if u == 0:
                        pe.wait_ge(v_out, (t + 1) * 2 * NS - NS)
                    elif not isinstance(t, int):
                        pe.wait_ge(v_out, (t + 1) * 2 * NS)
                for s in range(NS):
                    for j in range(2):
                        h = 2 * u + j
                        ins = nc.tensor.matmul(OB[64 * j:64 * j + 64, (u % 4) * N:(u % 4 + 1) * N],
                                               v[:, s, h * DH:(h + 1) * DH], PT[:, u % 2, j, s, :],
                                               start=(s == 0), stop=(s == NS - 1))
                ins.then_inc(av_done, 1)

            def project(t, part):
                if part == 0:
                    pe.wait_ge(o_out, 1 + 2 * (t + 2))
                    pe.wait_ge(y_out, t + 2)
                for u in range(2 * part, 2 * part + 2):
                    ins = nc.tensor.matmul(YB[0:N, 0:D], oT[:, u, :], wo[:, u, :], start=(u == 0), stop=(u == NP - 1))
                if part == 3:
                    ins.then_inc(y_done, 1)

            pe.wait_ge(ln.full_done, KT)
            for u in range(2):
                keys(0, u, PJ[u])
            pe.wait_ge(w_lo, 2)
            pe.wait_ge(init, 7)
            pe.wait_ge(wo_in, 16)
            with pe.Fori(0, NG) as g:
                pe.wait_ge(ln.lo_done, (g + 1) * KT)
                pe.wait_ge(k_lo, g * GB * NP + 2)
                for i in range(NP):
                    if i >= 2:
                        pe.wait_ge((q_act, q_dve)[i % 2], g * (NP // 2) + i // 2)
                    m = slice(128 * i, 128 * (i + 1))
                    mm3(nc, PJ[i % 2][:, 0:GT], lambda t: wqh[:, t, m], lambda t: wql[:, t, m],
                        lambda t: ln.hi[:, t, :], lambda t: ln.lo[:, t, :], KT).then_inc(q_mm, 1)
                pe.wait_ge(q_act, (g + 1) * (NP // 2))
                pe.wait_ge(q_dve, (g + 1) * (NP // 2))
                ln.pe_turn(nc, pe, k, g + 1, PJ)
                pe.wait_ge(w_lo, 3)
                with pe.Fori(0, GB) as b:
                    t = g * GB + b
                    pe.wait_ge(ln.full_done, (g + 2) * KT)
                    for u in range(NP):
                        turn(t if u >= LAG else t - 1, (u - LAG) % NP)
                        if u == NP - 2:
                            pe.wait_ge(k_lo, t * NP + NP)
                            pe.wait_ge(v_out, (t + 1) * 2 * NS)
                            cx.pe_turn(nc, pe, k, t + 1, PJ)
                        if u == LAG + 1:
                            scores(t, u)
                        values(t if u > LAG else t - 1, (u - LAG - 1) % NP)
                        if u != LAG + 1:
                            scores(t, u)
                        if u < NP - 2:
                            pe.wait_ge(k_lo, t * NP + (1 if u == 0 else u + 2))
                            keys(t, u + 2, PJ[0])
                            if u == 0:
                                pe.wait_ge(k_lo, t * NP + 2)
                            else:
                                pe.wait_ge(v_out, t * 2 * NS + u)
                            new_values(t, u)
                        if u == NP - 1:
                            pe.wait_ge(cx.lo_done, 2 * (t + 2))
                            for w in range(2):
                                keys(t + 1, w, PJ[w])
                        if LAG < u <= LAG + 4:
                            project(t - 1, u - LAG - 1)
            for i in range(LAG + 1):
                if i < LAG:
                    turn(B - 1, NP - LAG + i)
                values(B - 1, NP - LAG - 1 + i)
            for part in range(4):
                project(B - 1, part)


def feed_forward(nc, k, a, nxt, p, gated, load_out, wp_raw, wf_raw, wp_name, wf_name, cols, src, gain, shift):
    with ExitStack() as ctx:
        sb = lambda name, shape, dt=F32: ctx.enter_context(nc.sbuf_tensor(p + name, shape, dt))
        sem = phase_semaphores(k, 0)
        HT = FF // 128
        NW = 2 * FF if gated else FF
        bp, bf = k.consts[:, cols[0]:cols[0] + NW // 128], k.consts[:, cols[1]:cols[1] + KT]
        wph, wpl = sb("wp_hi", [128, KT, NW], F32R), sb("wp_lo", [128, KT, NW], F32R)
        wfh, wfl = sb("wf_hi", [128, HT, D], F32R), sb("wf_lo", [128, HT, D], F32R)
        ln = LN(nc, sb, sem, "", src, gain, shift)
        hi, lo = [[b, sb("xT_odd" + n, [128, KT, GT], F32R)] for b, n in ((ln.hi, "_hi"), (ln.lo, "_lo"))]
        gl = sb("gelu", [128, 2, GT])
        ph = sb("hidden_hi", [128, 2, GT], F32R)
        pl = sb("hidden_lo", [128, 2, GT], F32R)
        pf = sb("hidden", [128, 2, GT]) if gated else gl
        yT = sb("yT", [128, KT, GT])
        AB, GBK, YB, TB = k.bank[0:2], k.bank[2:4], k.bank[4:6], k.bank[6:8]
        w_hi, w_lo, wf_hi, wf_lo = sem("w_hi"), sem("w_lo"), sem("wf_hi"), sem("wf_lo")
        a_mm, g_mm, y_mm = sem("value_mm"), sem("gate_mm"), sem("y_mm")
        gelu_done, h_done, hh_done, hl_done = sem("gelu_done"), sem("hidden_done"), sem("hidden_hi"), sem("hidden_lo")
        yT_done, y_turned, x_done = sem("yT_done"), sem("y_turned"), sem("x_done")
        QW = 4
        parts = []
        for i in range(QW // 2):
            for half in ((0, 1) if gated else (0,)):
                w = FF // (QW // 2)
                parts.append(slice(half * FF + i * w, half * FF + (i + 1) * w))

        block = ctx.enter_context(nc.Block(no_gpsimd_drain=True))

        @block.sync
        def _(sp):
            sp.wait_ge(w_hi, len(parts))
            sp.wait_ge(w_lo, len(parts))
            sp.wait_ge(wf_hi, 1)
            sp.wait_ge(wf_lo, 1)
            nxt(sp)
            clear_semaphores(sp, k, 1)
            if load_out is not None:
                ov = load_out.rearrange("b n d -> n b d")
                with sp.Fori(0, NG) as g:
                    sp.wait_ge(x_done, 2 * (g + 1))
                    sp.dma_start(ov[:, bass.ds(g * GB, GB), :], k.x[:, bass.ds(g * GB + 1, GB), :]
                                 ).then_inc(k.out_done, 16)
                sp.wait_ge(k.out_done, NG * 16)

        @block.gpsimd
        def _(pool):
            ln.pool_rstd(nc, pool, k, 0)
            with pool.Fori(0, NG) as g:
                ln.pool_rstd(nc, pool, k, g + 1)

        @block.scalar
        def _(act):
            act.wait_ge(k.w_in[wp_name], 16)
            for i, c in enumerate(parts):
                nc.scalar.activation(wph[:, :, c], wp_raw[:, :, c], ACT.Copy).then_inc(w_hi, 1)
                if i == (1 if gated else 0):
                    ln.act_full(nc, act, 0, TB)
            act.wait_ge(k.w_in[wf_name], 16)
            nc.scalar.activation(wfh[:, :, :], wf_raw, ACT.Copy).then_inc(wf_hi, 1)

            def hidden(g, j):
                act.wait_ge(g_mm, g * HT + j + 1)
                if not (isinstance(g, int) and j == 0):
                    act.wait_ge(h_done if gated else hl_done, g * HT + j - 1)
                nc.scalar.activation(gl[:, j % 2, :], GBK[j % 2][:, 0:GT], ACT.Gelu,
                                     bias=bp[:, NW // 128 - HT + j:NW // 128 - HT + j + 1]).then_inc(gelu_done, 1)

            def round_hidden(g, j):
                act.wait_ge(y_mm, g * HT + j - 1 if j > 1 else g * HT)
                act.wait_ge(h_done if gated else gelu_done, g * HT + j + 1)
                nc.scalar.activation(ph[:, j % 2, :], pf[:, j % 2, :], ACT.Copy).then_inc(hh_done, 1)

            hidden(0, 0)
            with act.Fori(0, NG // 2) as pair:
                for odd in range(2):
                    g = 2 * pair + odd
                    for j in range(HT):
                        round_hidden(g, j)
                        if j < HT - 1:
                            hidden(g, j + 1)
                        else:
                            hidden(g + 1, 0)
                        if j == HT // 2 + 1:
                            ln.act_full(nc, act, g + 1, TB)
                        if j == HT // 2 + 2:
                            for t in range(KT):
                                act.wait_ge(ln.full_done, (g + 1) * KT + t + 1)
                                act.wait_ge(g_mm, g * HT)
                                nc.scalar.activation(hi[1 - odd][:, t, :], ln.yf[:, t, :], ACT.Copy
                                                     ).then_inc(ln.hi_done, 1)
                    act.wait_ge(y_mm, (g + 1) * HT)
                    for m in range(KT):
                        act.wait_ge(y_turned, g * GB)
                        nc.scalar.activation(yT[:, m, :], YB[m][:, 0:GT], ACT.Identity, bias=bf[:, m:m + 1]
                                             ).then_inc(yT_done, 1)

        @block.vector
        def _(dve):
            for b in range(GB):
                ln.dve_stats(nc, dve, 0, b)
            ln.dve_mean(nc, dve, 0, True)
            for b in range(GB):
                ln.dve_norm(nc, dve, 0, b, True)
            for i, c in enumerate(parts):
                dve.wait_ge(w_hi, i + 1)
                nc.vector.tensor_tensor(wpl[:, :, c], wp_raw[:, :, c], f32(wph[:, :, c]), ALU.subtract).then_inc(w_lo, 1)
                if i == (1 if gated else 0):
                    ln.split(nc.vector, k, 0)
            dve.wait_ge(wf_hi, 1)
            nc.vector.tensor_tensor(wfl[:, :, :], wf_raw, f32(wfh[:, :, :]), ALU.subtract).then_inc(wf_lo, 1)

            def hidden(g, j):
                if not gated:
                    return
                dve.wait_ge(gelu_done, g * HT + j + 1)
                if not (isinstance(g, int) and j == 0):
                    dve.wait_ge(hl_done, g * HT + j - 1)
                nc.vector.scalar_tensor_tensor(pf[:, j % 2, :], AB[j % 2][:, 0:GT], bp[:, j:j + 1], gl[:, j % 2, :],
                                               ALU.add, ALU.mult).then_inc(h_done, 1)

            def rest(g, j):
                dve.wait_ge(hh_done, g * HT + j + 1)
                nc.vector.tensor_tensor(pl[:, j % 2, :], pf[:, j % 2, :], f32(ph[:, j % 2, :]), ALU.subtract
                                        ).then_inc(hl_done, 1)

            hidden(0, 0)
            with dve.Fori(0, NG // 2) as pair:
                for odd in range(2):
                    g = 2 * pair + odd
                    for j in range(HT):
                        rest(g, j)
                        if j < HT - 1:
                            hidden(g, j + 1)
                        else:
                            hidden(g + 1, 0)
                        if j < 2:
                            ln.dve_stats(nc, dve, g + 1, 2 * j)
                            ln.dve_stats(nc, dve, g + 1, 2 * j + 1)
                        if j == 1:
                            ln.dve_mean(nc, dve, g + 1)
                        if j in (2, 3):
                            for b in range(2 * j - 4, 2 * j - 2):
                                ln.dve_norm(nc, dve, g + 1, b)
                        if j == HT // 2 + 2:
                            for t in range(KT):
                                dve.wait_ge(ln.hi_done, (g + 1) * KT + t + 1)
                                nc.vector.tensor_tensor(lo[1 - odd][:, t, :], ln.yf[:, t, :],
                                                        f32(hi[1 - odd][:, t, :]), ALU.subtract
                                                        ).then_inc(ln.lo_done, 1)
                    for i in range(GB // 2):
                        dve.wait_ge(y_turned, g * GB + 2 * i + 2)
                        xt = k.x[:, bass.ds(g * GB + 2 * i + 1, 2), :].rearrange("p a d -> p (a d)")
                        nc.vector.tensor_tensor(xt, xt, TB[i][0:N, :], ALU.add).then_inc(x_done, 1)

        @block.tensor
        def _(pe):
            ln.pe_turn(nc, pe, k, 0, TB)
            pe.wait_ge(ln.lo_done, KT)

            def product(g, j, odd):
                first = isinstance(g, int) and j == 0
                for bank, at, used, done in ((AB, 128 * j, h_done, a_mm), (GBK, NW - FF + 128 * j, gelu_done, g_mm)):
                    if done is a_mm and not gated:
                        continue
                    if not first:
                        pe.wait_ge(used, g * HT + j - 1)
                    m = slice(at, at + 128)
                    mm3(nc, bank[j % 2][:, 0:GT], lambda t: wph[:, t, m], lambda t: wpl[:, t, m],
                        lambda t: hi[odd][:, t, :], lambda t: lo[odd][:, t, :], KT).then_inc(done, 1)

            def output(g, j):
                pe.wait_ge(hl_done, g * HT + j + 1)
                if j == 0:
                    pe.wait_ge(yT_done, g * KT)
                for m in range(KT):
                    c = slice(128 * m, 128 * (m + 1))
                    for i, (w, h) in enumerate(((wfh, ph), (wfh, pl), (wfl, ph))):
                        ins = nc.tensor.matmul(YB[m][:, 0:GT], w[:, j, c], h[:, j % 2, :],
                                               start=(j == 0 and i == 0), stop=(j == HT - 1 and i == 2))
                ins.then_inc(y_mm, 1)

            pe.wait_ge(w_lo, len(parts) // 2)
            product(0, 0, 0)
            with pe.Fori(0, NG // 2) as pair:
                for odd in range(2):
                    g = 2 * pair + odd
                    for j in range(HT):
                        if j == HT // 2 - 1:
                            pe.wait_ge(w_lo, len(parts))
                        if j < HT - 1:
                            product(g, j + 1, odd)
                        else:
                            pe.wait_ge(ln.lo_done, (g + 2) * KT)
                            product(g + 1, 0, 1 - odd)
                        if j == 0:
                            pe.wait_ge(wf_lo, 1)
                        output(g, j)
                        if j == HT // 2:
                            pe.wait_ge(x_done, 2 * g)
                            ln.pe_turn(nc, pe, k, g + 1, TB)
                    pe.wait_ge(ln.full_done, (g + 2) * KT)
                    pe.wait_ge(yT_done, (g + 1) * KT)
                    for b in range(GB):
                        for m in range(KT):
                            ins = nc.tensor.transpose(TB[b // 2][0:N, (b % 2) * D + 128 * m:(b % 2) * D + 128 * (m + 1)],
                                                      yT[:, m, b * N:(b + 1) * N], k.ident[:, :])
                        ins.then_inc(y_turned, 1)


def narrow_attention(nc, k, a, nxt):
    with ExitStack() as ctx:
        sb = lambda name, shape, dt=F32: ctx.enter_context(nc.sbuf_tensor("D_" + name, shape, dt))
        sem = phase_semaphores(k, 1)
        LAG = 2
        MT, SLOTS = H // 4, 2 * D
        wqh, wkh = [sb(f"w{w}_hi", [128, 2, SLOTS], F32R) for w in "qk"]
        wql, wkl = [sb(f"w{w}_lo", [128, 2, SLOTS], F32R) for w in "qk"]
        wvh, wvl = sb("wv_hi", [128, 2, D], F32R), sb("wv_lo", [128, 2, D], F32R)
        wo = sb("wo", [128, MT, D])
        ln = LN(nc, sb, sem, "", k.x, None, None, norm=False)
        lowhalf, bq, bk, bv = k.consts[:, 0:1], k.consts[:, 45:49], k.consts[:, 49:53], k.consts[:, 53:57]
        cx = Context(nc, sb, sem)
        qg = sb("q_group", [128, MT, GT])
        qh = sb("q_hi", [128, MT, N], F32R)
        ql = sb("q_lo", [128, MT, N], F32R)
        kf = sb("k_full", [128, SP])
        kr = sb("k_rounded", [128, SP], F32R)
        ks = sb("k_slots", [128, MT, SP], F32R)
        v = sb("v", [ST, NS, H, 2, DL])
        P = sb("probs", [N, 2, 2, SP])
        bqs = sb("bq_scaled", [128, MT])
        PT = sb("probsT", [ST, 2, 2, NS, N])
        oT = sb("oT", [128, MT, N])
        nm = sb("neg_max", [N, 2, 2])
        sm = sb("sums", [N, 2, 2])
        rc = sb("rsums", [N, 2, 2])
        SB, TB, OB, YB, PJ = k.bank[0:2], k.bank[2:4], k.bank[4], k.bank[5], k.bank[6:8]

        wo_in, w_hi, w_lo, init, wo_cleared = sem("wo_in"), sem("w_hi"), sem("w_lo"), sem("init"), sem("wo_cleared")
        q_mm, q_act, q_dve, qh_done, ql_done = sem("q_mm"), sem("q_act"), sem("q_dve"), sem("qh"), sem("ql")
        k_mm, k_full, k_round, k_lo = sem("k_mm"), sem("k_full_done"), sem("k_rounded_done"), sem("k_slots_done")
        v_mm, v_out = sem("v_mm"), sem("v_out")
        s_done, max_done, exp_done = sem("scores_done"), sem("max_done"), sem("exp_done")
        rcp_done, norm_done, t_done = sem("rcp_done"), sem("norm_done"), sem("turned")
        pt_out, av_done, o_out = sem("probsT_out"), sem("av_done"), sem("oT_out")
        y_done, y_out, x_done, bqs_set = sem("y_done"), sem("y_out"), sem("x_done"), sem("bq_scaled")
        EXP0, NORM0, T0, PT0, AV0, O0, Y0 = 2, NP, 2 + NP - LAG, 2 * (1 + NP - LAG), 2 + NP - LAG - 1, 2 * (1 + 1), 1

        block = ctx.enter_context(nc.Block(no_gpsimd_drain=True))

        @block.sync
        def _(sp):
            sp.wait_ge(cx.cleared, 1)
            wos = a["L1_xattn_Wo"].rearrange("(m s d) n -> s d m n", s=4, d=DL)
            sp.wait_ge(wo_cleared, 1)
            for s in range(4):
                sp.dma_start(wo[32 * s:32 * s + DL, :, :], wos[s, :, :, :]).then_inc(wo_in, 16)
            cx.load(sp, a["ctx_768"], 0)
            nxt(sp)
            clear_semaphores(sp, k, 0)
            cx.sp_loop(sp, a["ctx_768"])
            sp.wait_ge(ln.lo_done, (NG + 1) * KT)

        @block.gpsimd
        def _(pool):
            nc.gpsimd.memset(cx.raw[:, :, :], 0.0).then_inc(cx.cleared, 1)
            nc.gpsimd.memset(wo[:, :, :], 0.0).then_inc(wo_cleared, 1)
            nc.gpsimd.memset(k.y[:, 1 + B:1 + B + GB, :], 0.0).then_inc(k.ypad_set, 1)
            nc.gpsimd.memset(P[:, :, :, :], 0.0).then_inc(init, 1)
            nc.gpsimd.memset(PT[:, :, :, :, :].rearrange("p r j s n -> p (r j s n)"), 0.0).then_inc(init, 1)
            nc.gpsimd.memset(oT[:, :, :], 0.0).then_inc(init, 1)
            with pool.Fori(0, NG) as g:
                for b in range(GB):
                    t = g * GB + b
                    pool.wait_ge(q_act, (g + 1) * (MT // 2))
                    pool.wait_ge(q_dve, (g + 1) * (MT // 2))
                    for u in range(MT):
                        pool.wait_ge(s_done, 2 * (t * NP + 2 * u + 2))
                        nc.gpsimd.tensor_tensor(qh[:, u, :], qg[:, u, b * N:(b + 1) * N],
                                                k.ones[:, :].to_broadcast([128, N]), ALU.mult
                                                ).then_inc(qh_done, 1)
                        pool.wait_ge(qh_done, t * MT + u + 1)
                        nc.gpsimd.tensor_tensor(ql[:, u, :], qg[:, u, b * N:(b + 1) * N], f32(qh[:, u, :]),
                                                ALU.subtract).then_inc(ql_done, 1)
                ln.split(nc.gpsimd, k, g + 1)

        @block.scalar
        def _(act):
            raws = {w: k.stage[:, 2, 512 * i:512 * (i + 1)].rearrange("p (t n) -> p t n", t=2) for i, w in enumerate("qkv")}

            def twice(w):
                return raws[w].rearrange("p t (h d) -> p (t h) d", d=DL).unsqueeze(2).to_broadcast([128, 2 * H, 2, DL])

            for i, (w, src) in enumerate(((wkh, "k"), (wqh, "q"))):
                act.wait_ge(k.w_in[f"L1_xattn_W{src}"], (CONTEXT_LOADS, 16)[i])
                nc.scalar.activation(w[:, :, :].rearrange("p t (h r d) -> p (t h) r d", r=2, d=DL), twice(src), ACT.Copy
                                     ).then_inc(w_hi, 1)
            act.wait_ge(k.w_in["L1_xattn_Wv"], CONTEXT_LOADS)
            nc.scalar.activation(wvh[:, :, :], raws["v"], ACT.Copy).then_inc(w_hi, 1)
            cx.act_hi(nc, act, 0, k.bank[2:4])
            ln.act_full(nc, act, 0, PJ)
            act.sem_inc(o_out, O0)
            act.sem_inc(exp_done, EXP0)
            act.sem_inc(pt_out, PT0)

            def exps(t, u):
                act.wait_ge(t_done, (t + 1) * NP + u + 1)
                for j in range(2):
                    act.wait_ge(max_done, 2 * (t * NP + u) + j + 1)
                    nc.scalar.activation(P[:, u % 2, j, 0:S], SB[j][0:N, 0:S], ACT.Exp, bias=nm[:, u % 2, j:j + 1],
                                         accum_out=sm[:, u % 2, j:j + 1]).then_inc(exp_done, 1)

            def pt_evac(t, u):
                act.wait_ge(t_done, 2 + (t + 1) * NP + u + 1)
                act.wait_ge(av_done, (t + 1) * NP + u + 1)
                for j in range(2):
                    nc.scalar.activation(PT[:, u % 2, j, :, :].rearrange("p s n -> p (s n)"), TB[j][0:ST, 0:NS * N],
                                         ACT.Copy).then_inc(pt_out, 1)

            def o_evac(t, h):
                act.wait_ge(av_done, 2 + (t + 1) * NP + 4 * h + 4)
                act.wait_ge(y_done, t + 1)
                for m in range(2 * h, 2 * h + 2):
                    nc.scalar.activation(oT[:, m, :], OB[:, m * N:(m + 1) * N], ACT.Identity, bias=bv[:, m:m + 1]
                                         ).then_inc(o_out, 1)

            def keys(t, m):
                act.wait_ge(k_mm, t * MT + m + 1)
                act.wait_ge(k_lo, t * MT + m)
                nc.scalar.activation(kf[:, :], PJ[0][:, 0:SP], ACT.Identity, bias=bk[:, m:m + 1]).then_inc(k_full, 1)

            def new_values(t, s):
                act.wait_ge(v_mm, t * NS + s + 1)
                src = PJ[1 - s % 2][0:ST, 0:D].rearrange("p (h d) -> p h d", d=DL).unsqueeze(2).to_broadcast([ST, H, 2, DL])
                nc.scalar.activation(v[:, s, :, :, :], src, ACT.Copy).then_inc(v_out, 1)

            keys(0, 0)
            act.wait_ge(bqs_set, 1)
            with act.Fori(0, NG) as g:
                for i in range(0, MT, 2):
                    act.wait_ge(q_mm, g * MT + i + 1)
                    act.wait_ge(ql_done, g * GB * MT)
                    nc.scalar.activation(qg[:, i, :], PJ[0][:, 0:GT], ACT.Identity, bias=bqs[:, i:i + 1],
                                         scale=DL ** -0.5).then_inc(q_act, 1)
                ln.act_full(nc, act, g + 1, PJ)
                with act.Fori(0, GB) as b:
                    t = g * GB + b
                    for u in range(NP):
                        pt_evac(t if u >= LAG else t - 1, (u - LAG) % NP)
                        if u == NP - 2:
                            o_evac(t, 0)
                        exps(t, u)
                        if u == 1:
                            o_evac(t - 1, 1)
                            new_values(t, 0)
                            new_values(t, 1)
                        if u == 2:
                            new_values(t, 2)
                        if u in (0, 2, 4):
                            keys(t, u // 2 + 1)
                        if u == NP - 3:
                            cx.act_hi(nc, act, t + 1, PJ)
                        if u == NP - 1:
                            keys(t + 1, 0)
            for u in range(NP - LAG, NP):
                pt_evac(B - 1, u)
            o_evac(B - 1, 1)

        @block.vector
        def _(dve):
            dve.sem_inc(y_out, Y0)
            dve.sem_inc(norm_done, NORM0)
            nc.vector.tensor_scalar(bqs[:, :], bq, DL ** -0.5, None, ALU.mult).then_inc(bqs_set, 1)
            for b in range(GB):
                ln.dve_norm(nc, dve, 0, b, True)
            for w in (wkl, wvl):
                nc.vector.memset(f32(w[CR:128, 1, :]), 0.0).then_inc(init, 1)
            nc.vector.memset(v[:, :, :, :, :].rearrange("p s h r d -> p (s h r d)"), 0.0).then_inc(init, 1)
            nc.vector.memset(OB[:, 0:4 * N], 0.0).then_inc(init, 1)
            raws = {w: k.stage[:, 2, 512 * i:512 * (i + 1)].rearrange("p (t n) -> p t n", t=2) for i, w in enumerate("qkv")}
            for i, (w, wh, src, rows) in enumerate(((wkl, wkh, "k", CR), (wql, wqh, "q", 128), (wvl, wvh, "v", CR))):
                dve.wait_ge(w_hi, i + 1)
                for t, r in ((0, 128), (1, rows)):
                    if src == "v":
                        ins = nc.vector.tensor_tensor(w[0:r, t, :], raws[src][0:r, t, :], f32(wh[0:r, t, :]), ALU.subtract)
                    else:
                        raw = raws[src][0:r, t, :].rearrange("p (h d) -> p h d", d=DL)
                        slots = lambda x: x[0:r, t, :].rearrange("p (h r d) -> p h r d", r=2, d=DL)
                        for twice in range(2):
                            ins = nc.vector.tensor_tensor(slots(w)[:, :, twice, :], raw, f32(slots(wh)[:, :, twice, :]),
                                                          ALU.subtract)
                    ins.then_inc(w_lo, 1)
                if i == 0:
                    cx.dve_lo(nc, dve, 0, k.bank[2:4])
                    ln.split(nc.vector, k, 0)
            dve.wait_ge(init, 7)

            def maxima(t, u):
                for j in range(2):
                    dve.wait_ge(s_done, 2 * (NP + t * NP + u) + j + 1)
                    nc.vector.tensor_reduce(nm[:, u % 2, j:j + 1], SB[j][0:N, 0:S], AX.X, ALU.max, negate=True
                                            ).then_inc(max_done, 1)

            def norm(t, u):
                dve.wait_ge(exp_done, EXP0 + t * 2 * NP + 2 * u + 2)
                nc.vector.reciprocal(rc[:, u % 2, :], sm[:, u % 2, :]).then_inc(rcp_done, 1)
                dve.wait_ge(rcp_done, t * NP + u + 1)
                nc.vector.tensor_tensor(P[:, u % 2, :, 0:S], P[:, u % 2, :, 0:S],
                                        rc[:, u % 2, :].unsqueeze(2).to_broadcast([N, 2, S]),
                                        ALU.mult).then_inc(norm_done, 1)

            def keys(t, m):
                dve.wait_ge(k_full, t * MT + m + 1)
                nc.vector.tensor_copy(kr[:, :], kf[:, :]).then_inc(k_round, 1)
                dve.wait_ge(k_round, t * MT + m + 1)
                nc.vector.scalar_tensor_tensor(ks[:, m, :], f32(kr[:, :]), lowhalf, kf[:, :], ALU.mult, ALU.add
                                               ).then_inc(k_lo, 1)

            def x_update(t):
                dve.wait_ge(y_done, t + 2)
                dve.wait_ge(x_done, t + 1)
                yt = k.y[:, bass.ds(t + 1, 1), :].rearrange("p a d -> p (a d)")
                nc.vector.tensor_tensor(yt, YB[0:N, 0:D], k.bcast[:, 2, :], ALU.add).then_inc(y_out, 1)
                dve.wait_ge(y_out, Y0 + t + 2)
                xt = k.x[:, bass.ds(t + 1, 1), :].rearrange("p a d -> p (a d)")
                nc.vector.tensor_tensor(xt, xt, yt, ALU.add).then_inc(x_done, 1)

            keys(0, 0)
            with dve.Fori(0, NG) as g:
                for i in range(MT):
                    ln.dve_norm(nc, dve, g + 1, i)
                    if i % 2:
                        dve.wait_ge(q_mm, g * MT + i + 1)
                        dve.wait_ge(ql_done, g * GB * MT)
                        nc.vector.tensor_scalar(qg[:, i, :], PJ[1][:, 0:GT], bq[:, i:i + 1], DL ** -0.5, ALU.add,
                                                ALU.mult).then_inc(q_dve, 1)
                with dve.Fori(0, GB) as b:
                    t = g * GB + b
                    for u in range(NP):
                        if u > 0:
                            norm(t, u - 1)
                        maxima(t, u)
                        if u in (0, 2, 4):
                            keys(t, u // 2 + 1)
                        if u == NP - 2:
                            cx.dve_lo(nc, dve, t + 1, PJ)
                        if u == NP - 1:
                            keys(t + 1, 0)
                    norm(t, NP - 1)
                    x_update(t - 1)
            x_update(B - 1)

        @block.tensor
        def _(pe):
            cx.pe_turn(nc, pe, k, 0, k.bank[2:4])
            ln.pe_turn(nc, pe, k, 0, PJ)
            pe.sem_inc(t_done, T0)
            pe.sem_inc(av_done, AV0)
            pe.sem_inc(s_done, 2 * NP)
            pe.wait_ge(w_lo, 2)
            pe.wait_ge(cx.lo_done, 2)

            def keys(t, m):
                c = slice(128 * m, 128 * (m + 1))
                mm5(nc, PJ[0][:, 0:SP], ([wkh[:, i, c] for i in range(2)], [wkl[:, i, c] for i in range(2)]),
                    cx.cols(slice(0, SP)), False).then_inc(k_mm, 1)

            def new_values(t, s):
                mm5(nc, PJ[1 - s % 2][0:ST, 0:D], cx.cols(slice(ST * s, ST * (s + 1))),
                    ([wvh[:, i, :] for i in range(2)], [wvl[:, i, :] for i in range(2)]), True).then_inc(v_mm, 1)

            def scores(t, u):
                if u % 2 == 0:
                    pe.wait_ge(ql_done, t * MT + u // 2 + 1)
                    pe.wait_ge(k_lo, t * MT + u // 2 + 1)
                for i, x in enumerate((qh, ql)):
                    for j in range(2):
                        if i == 0:
                            pe.wait_ge(exp_done, 2 * (t * NP + u) + j + 1)
                        r = slice(32 * (2 * (u % 2) + j), 32 * (2 * (u % 2) + j) + 32)
                        ins = nc.tensor.matmul(SB[j][0:N, 0:SP], x[r, u // 2, :], ks[r, u // 2, :],
                                               start=(i == 0), stop=(i == 1), tile_position=(r.start, 0))
                        if i == 1:
                            ins.then_inc(s_done, 1)

            def turn(t, u):
                pe.wait_ge(norm_done, (t + 1) * NP + u + 1)
                pe.wait_ge(pt_out, 2 * ((t + 1) * NP + u + 1))
                for j in range(2):
                    for s in range(NS):
                        ins = nc.tensor.transpose(TB[j][0:ST, s * N:(s + 1) * N],
                                                  P[:, u % 2, j, ST * s:ST * (s + 1)], k.ident[0:N, 0:N])
                ins.then_inc(t_done, 1)

            def values(t, u):
                pe.wait_ge(pt_out, 2 * (1 + (t + 1) * NP + u + 1))
                if u % 4 == 0:
                    pe.wait_ge(o_out, 2 * ((t + 1) * 2 + u // 4 + 1))
                    if u == 0:
                        pe.wait_ge(v_out, (t + 1) * NS)
                for s in range(NS):
                    for j in range(2):
                        h = 2 * u + j
                        r = 32 * (h % 4)
                        ins = nc.tensor.matmul(OB[r:r + 32, (h // 4) * N:(h // 4 + 1) * N],
                                               v[:, s, h, :, :].rearrange("p r d -> p (r d)"), PT[:, u % 2, j, s, :],
                                               start=(s == 0), stop=(s == NS - 1), tile_position=(0, r))
                ins.then_inc(av_done, 1)

            def project(t):
                pe.wait_ge(o_out, 2 * (1 + 2 * (t + 2)))
                pe.wait_ge(y_out, t + 2)
                for m in range(MT):
                    ins = nc.tensor.matmul(YB[0:N, 0:D], oT[:, m, :], wo[:, m, :], start=(m == 0), stop=(m == MT - 1))
                ins.then_inc(y_done, 1)

            pe.wait_ge(ln.full_done, KT)
            keys(0, 0)
            pe.wait_ge(w_lo, 6)
            pe.wait_ge(init, 7)
            pe.wait_ge(wo_in, 64)
            with pe.Fori(0, NG) as g:
                pe.wait_ge(ln.lo_done, (g + 1) * KT)
                pe.wait_ge(k_lo, g * GB * MT + 1)
                pe.wait_ge(cx.lo_done, 2 * (g * GB + 1))
                for i in range(MT):
                    if i >= 2:
                        pe.wait_ge((q_act, q_dve)[i % 2], g * (MT // 2) + i // 2)
                    m = slice(128 * i, 128 * (i + 1))
                    mm3(nc, PJ[i % 2][:, 0:GT], lambda t: wqh[:, t, m], lambda t: wql[:, t, m],
                        lambda t: ln.hi[:, t, :], lambda t: ln.lo[:, t, :], KT).then_inc(q_mm, 1)
                pe.wait_ge(q_act, (g + 1) * (MT // 2))
                pe.wait_ge(q_dve, (g + 1) * (MT // 2))
                ln.pe_turn(nc, pe, k, g + 1, PJ)
                with pe.Fori(0, GB) as b:
                    t = g * GB + b
                    pe.wait_ge(ln.full_done, (g + 2) * KT)
                    for u in range(NP):
                        turn(t if u >= LAG else t - 1, (u - LAG) % NP)
                        if u != LAG:
                            values(t if u > LAG else t - 1, (u - LAG - 1) % NP)
                        scores(t, u)
                        if u == 1:
                            values(t - 1, NP - 1)
                        if u == 1:
                            new_values(t, 0)
                            pe.wait_ge(k_lo, t * MT + 2)
                            new_values(t, 1)
                        if u == 2:
                            pe.wait_ge(v_out, t * NS + 2)
                            new_values(t, 2)
                        if u in (0, 2, 4):
                            pe.wait_ge(k_lo, t * MT + u // 2 + 1)
                            keys(t, u // 2 + 1)
                        if u == NP - 3:
                            pe.wait_ge(k_lo, t * MT + MT)
                            pe.wait_ge(v_out, (t + 1) * NS)
                            cx.pe_turn(nc, pe, k, t + 1, PJ)
                        if u == NP - 1:
                            pe.wait_ge(cx.lo_done, 2 * (t + 2))
                            keys(t + 1, 0)
                        if u == LAG:
                            project(t - 1)
            for i in range(LAG):
                turn(B - 1, NP - LAG + i)
                values(B - 1, NP - LAG - 1 + i)
            values(B - 1, NP - 1)
            project(B - 1)


def program(nc, a, out):
    with ExitStack() as ctx:
        k = Core()
        resident(nc, ctx, k)
        k.shared = ({}, {})
        k.c_in, k.rows_in, k.out_done = k.sem("vectors_in"), k.sem("rows_in"), k.sem("out_done")
        k.x_in, k.w_in = [k.sem(f"x_in{i}") for i in range(2)], {w: k.sem(f"{w}_in") for w in WEIGHTS}
        k.half_set, k.ident_set, k.pad_set = k.sem("half_set"), k.sem("ident_set"), k.sem("pad_set")
        k.mask_set, k.cols_turned, k.cols_set = k.sem("mask_set"), k.sem("cols_turned"), k.sem("cols_set")
        k.ypad_set = k.sem("ypad_set")

        def plain(sp, dst, name, sem):
            t = a[name].shape[0] // 128
            sp.dma_start(dst.rearrange("p (t n) -> p t n", t=t), a[name].rearrange("(t p) n -> p t n", p=128)
                         ).then_inc(sem, 16)

        stage = k.stage[:, :, :].rearrange("p w n -> p (w n)")

        def weights_b(sp):
            plain(sp, k.stage[:, 0, :], "L0_xattn_Wq2", k.w_in["L0_xattn_Wq2"])
            context_weights_in(sp, k.stage[:, 1, :], a["L0_xattn_Wk2"], k.w_in["L0_xattn_Wk2"])
            context_weights_in(sp, k.stage[:, 2, :], a["L0_xattn_Wv2"], k.w_in["L0_xattn_Wv2"])

        def weights_c(sp):
            plain(sp, stage[:, 0:4096], "L0_xattn_Wp", k.w_in["L0_xattn_Wp"])
            plain(sp, stage[:, 4096:6144], "L0_xattn_Wf", k.w_in["L0_xattn_Wf"])

        def weights_de(sp):
            plain(sp, stage[:, 4096:4608], "L1_xattn_Wq", k.w_in["L1_xattn_Wq"])
            context_weights_in(sp, stage[:, 4608:5120], a["L1_xattn_Wk"], k.w_in["L1_xattn_Wk"])
            context_weights_in(sp, stage[:, 5120:5632], a["L1_xattn_Wv"], k.w_in["L1_xattn_Wv"])
            plain(sp, stage[:, 0:2048], "L1_xattn_W1", k.w_in["L1_xattn_W1"])
            plain(sp, stage[:, 2048:4096], "L1_xattn_W2", k.w_in["L1_xattn_W2"])

        def cut(lo, hi, t):
            return stage[:, lo:hi].rearrange("p (t n) -> p t n", t=t)

        none = lambda sp: None
        self_attention(nc, k, a, weights_b)
        cross_attention(nc, k, a, weights_c)
        feed_forward(nc, k, a, weights_de, "C_", True, None, cut(0, 4096, KT), cut(4096, 6144, FF // 128), "L0_xattn_Wp", "L0_xattn_Wf",
                     (13, 29), k.x, k.consts[:, 9:11], k.consts[:, 11:13])
        with nc.sbuf_tensor("y_tokens", [N, 1 + B + GB, D], F32) as y:
            k.y = y
            narrow_attention(nc, k, a, none)
            feed_forward(nc, k, a, none, "E_", False, out, cut(0, 2048, KT), cut(2048, 4096, FF // 128), "L1_xattn_W1", "L1_xattn_W2",
                         (35, 43), k.y, k.consts[:, 31:33], k.consts[:, 33:35])


_INS = [
    'x', 'ctx_768', 'L0_xattn_Wq1', 'L0_xattn_Wk1', 'L0_xattn_Wv1', 'L0_xattn_Wo1', 'L0_xattn_bo1',
    'L0_xattn_Wq2', 'L0_xattn_Wk2', 'L0_xattn_Wv2', 'L0_xattn_Wo2', 'L0_xattn_bo2', 'L0_xattn_Wp',
    'L0_xattn_bp', 'L0_xattn_Wf', 'L0_xattn_bf', 'L0_xattn_g1', 'L0_xattn_b1', 'L0_xattn_g2', 'L0_xattn_b2',
    'L0_xattn_g3', 'L0_xattn_b3', 'L1_xattn_Wq', 'L1_xattn_bq', 'L1_xattn_Wk', 'L1_xattn_bk', 'L1_xattn_Wv',
    'L1_xattn_bv', 'L1_xattn_Wo', 'L1_xattn_bo', 'L1_xattn_ln_g', 'L1_xattn_ln_b', 'L1_xattn_W1',
    'L1_xattn_b1', 'L1_xattn_W2', 'L1_xattn_b2',
]
_OUTS = [((16, 112, 256), "float32")]


def kernel(**inputs):
    import numpy as _np
    import concourse.bacc as _bacc
    from concourse import mybir as _mybir
    from concourse.bass_utils import run_bass_kernel_spmd as _run

    nc = _bacc.Bacc("TRN2", target_bir_lowering=False, num_devices=1)
    arrays, args = {}, {}
    for name in _INS:
        x = _np.ascontiguousarray(inputs[name])
        arrays[f"in_{name}_dram"] = x
        args[name] = nc.dram_tensor(f"in_{name}_dram", x.shape, _mybir.dt.from_np(x.dtype), kind="ExternalInput").ap()
    shape, dtype = _OUTS[0]
    out = nc.dram_tensor("out_0_dram", shape, _mybir.dt.from_np(_np.dtype(dtype)), kind="ExternalOutput").ap()
    program(nc, args, out)
    r = _run(nc, [arrays], core_ids=[0])
    return r.results[0]["out_0_dram"]
```

```python
from contextlib import ExitStack

import concourse.bass as bass
from concourse import mybir

F32 = mybir.dt.float32
F32R = mybir.dt.float32r
ALU = mybir.AluOpType
ACT = mybir.ActivationFunctionType
AX = mybir.AxisListType

B, N, D = 16, 112, 256
S, C = 375, 192
H = 16
NP = H // 2
DH = 64
INNER = H * DH
DL = D // H
FF = 4 * D
KT = D // 128
ST = 126
NS = 3
SP = NS * ST
CR = C - 128
GB = 4
NG = B // GB
GT = GB * N
EPS = 1e-5
LAG = 3
PS = 4


def f32(ap):
    return ap.bitcast(F32)


class Core:
    pass


def resident(nc, ctx, k):
    sb = lambda name, shape, dt=F32: ctx.enter_context(nc.sbuf_tensor(name, shape, dt))
    k.x = sb("x_tokens", [N, 1 + B + GB, D])
    k.ident = sb("ident", [128, 128])
    k.stage = sb("w_stage", [128, 3, 2048])
    k.ctx_raw = sb("ctx", [ST, NS, C])
    k.vrows = sb("vector_rows", [NCOL, 128])
    k.consts = sb("vector_columns", [128, NCOL])
    k.bcast = sb("bias_rows", [N, 3, D])
    k.half = sb("minus_half", [N, GB])
    k.eps = sb("eps", [N, GB])
    k.ones = sb("ones", [128, 1])
    k.bank = [ctx.enter_context(nc.psum_tensor(f"bank{i}", [128, 512], F32)) for i in range(8)]
    k.sem = lambda name: ctx.enter_context(nc.semaphore(name))


COLUMNS = {"L0_xattn_g1": 1, "L0_xattn_b1": 3, "L0_xattn_g2": 5, "L0_xattn_b2": 7, "L0_xattn_g3": 9,
           "L0_xattn_b3": 11, "L0_xattn_bp": 13, "L0_xattn_bf": 29, "L1_xattn_ln_g": 31,
           "L1_xattn_ln_b": 33, "L1_xattn_b1": 35, "L1_xattn_b2": 43}
SLOT_COLUMNS = {"L1_xattn_bq": 45, "L1_xattn_bk": 49, "L1_xattn_bv": 53}
NCOL = 57
ROWS = ["L0_xattn_bo1", "L0_xattn_bo2", "L1_xattn_bo"]
WEIGHTS = ["L0_xattn_Wq1", "L0_xattn_Wk1", "L0_xattn_Wv1", "L0_xattn_Wq2", "L0_xattn_Wk2", "L0_xattn_Wv2", "L0_xattn_Wp",
           "L0_xattn_Wf", "L1_xattn_Wq", "L1_xattn_Wk", "L1_xattn_Wv", "L1_xattn_W1", "L1_xattn_W2"]
VECTOR_LOADS = 16 * (len(COLUMNS) + 2 * len(SLOT_COLUMNS))
ROW_LOADS = 16 * len(ROWS)


def phase_semaphores(k, turn):
    def get(name):
        if name not in k.shared[turn]:
            k.shared[turn][name] = k.sem(("even_", "odd_")[turn] + name)
        return k.shared[turn][name]
    return get


def clear_semaphores(sp, k, turn):
    for s in k.shared[turn].values():
        sp.sem_clear(s)


def load_vectors(sp, k, a):
    for name, at in COLUMNS.items():
        n = a[name].shape[0] // 128
        sp.dma_start(k.vrows[at:at + n, :], a[name].rearrange("(c p) -> c p", p=128)).then_inc(k.c_in, 16)
    for name, at in SLOT_COLUMNS.items():
        for twice in range(2):
            sp.dma_start(k.vrows[at:at + 4, :].rearrange("m (s t d) -> m s t d", s=4, t=2)[:, :, twice, :],
                         a[name].rearrange("(m s d) -> m s d", s=4, d=DL)).then_inc(k.c_in, 16)


def load_rows(sp, k, a):
    for i, name in enumerate(ROWS):
        sp.dma_start(k.bcast[:, i, :], a[name].rearrange("(o n) -> o n", o=1).to_broadcast([N, D])
                     ).then_inc(k.rows_in, 16)


class LN:

    def __init__(self, nc, sb, sem, p, src, gain, shift, norm=True):
        self.src, self.gain, self.shift, self.norm = src, gain, shift, norm
        self.st = sb(p + "ln_stats", [N, GB, 6])
        self.mv = sb(p + "ln_mean_var", [N, GB, 2])
        self.ve = sb(p + "ln_var_eps", [N, GB])
        self.rs = sb(p + "ln_rstd", [N, GB])
        self.xh = sb(p + "ln_out", [N, GB, D])
        self.yf = sb(p + "xT", [128, KT, GT])
        self.hi = sb(p + "xT_hi", [128, KT, GT], F32R)
        self.lo = sb(p + "xT_lo", [128, KT, GT], F32R)
        self.stats_done = sem(p + "ln_stats_done")
        self.mean_done = sem(p + "ln_mean_done")
        self.stats_seen = sem(p + "ln_stats_seen")
        self.var_done = sem(p + "ln_var_done")
        self.rstd_done = sem(p + "ln_rstd_done")
        self.norm_done = sem(p + "ln_norm_done")
        self.turned = sem(p + "ln_turned")
        self.full_done = sem(p + "ln_full_done")
        self.hi_done = sem(p + "ln_hi_done")
        self.lo_done = sem(p + "ln_lo_done")

    def dve_stats(self, nc, dve, g, k):
        if not isinstance(g, int):
            dve.wait_ge(self.mean_done, g * GB)
        nc.vector.bn_stats(self.st[:, k, :], self.src[:, bass.ds(g * GB + k + 1, 1), :].rearrange("p a d -> p (a d)")
                           ).then_inc(self.stats_done, 1)

    def dve_mean(self, nc, dve, g, first=False):
        dve.wait_ge(self.stats_done, (g + 1) * GB)
        if not first:
            dve.wait_ge(self.norm_done, g * GB)
            dve.sem_inc(self.stats_seen, 1)
        for k in range(GB):
            nc.vector.bn_aggr(self.mv[:, k, :], self.st[:, k, :]).then_inc(self.mean_done, 1)

    def dve_norm(self, nc, dve, g, k, first=False):
        if not first:
            dve.wait_ge(self.turned, g * GB * KT)
        src = self.src[:, bass.ds(g * GB + k + 1, 1), :].rearrange("p a d -> p (a d)")
        if self.norm:
            dve.wait_ge(self.rstd_done, g + 1)
            nc.vector.tensor_scalar(self.xh[:, k, :], src, self.mv[:, k, 0:1], self.rs[:, k:k + 1],
                                    ALU.subtract, ALU.mult).then_inc(self.norm_done, 1)
        else:
            nc.vector.tensor_copy(self.xh[:, k, :], src).then_inc(self.norm_done, 1)

    def pool_rstd(self, nc, pool, k, g):
        pool.wait_ge(self.mean_done, (g + 1) * GB)
        if not isinstance(g, int):
            pool.wait_ge(self.norm_done, g * GB)
        nc.gpsimd.tensor_tensor(self.ve[:, :], self.mv[:, :, 1], k.eps[:, :], ALU.add).then_inc(self.var_done, 1)
        pool.wait_ge(self.var_done, g + 1)
        nc.gpsimd.tensor_tensor(self.rs[:, :], self.ve[:, :], k.half[:, :], ALU.pow).then_inc(self.rstd_done, 1)

    def pe_turn(self, nc, pe, k, g, banks):
        for b in range(GB):
            pe.wait_ge(self.norm_done, g * GB + b + 1)
            for t in range(KT):
                nc.tensor.transpose(banks[t][:, b * N:(b + 1) * N], self.xh[:, b, t * 128:(t + 1) * 128],
                                    k.ident[0:N, 0:N]).then_inc(self.turned, 1)

    def act_full(self, nc, act, g, banks):
        act.wait_ge(self.turned, (g + 1) * GB * KT)
        if not isinstance(g, int):
            act.wait_ge(self.lo_done, g * KT)
        for t in range(KT):
            if self.norm:
                ins = nc.scalar.activation(self.yf[:, t, :], banks[t][:, 0:GT], ACT.Identity,
                                           bias=self.shift[:, t:t + 1], scale=self.gain[:, t:t + 1])
            else:
                ins = nc.scalar.activation(self.yf[:, t, :], banks[t][:, 0:GT], ACT.Copy)
            ins.then_inc(self.full_done, 1)

    def act_round(self, nc, act, g):
        for t in range(KT):
            act.wait_ge(self.full_done, g * KT + t + 1)
            nc.scalar.activation(self.hi[:, t, :], self.yf[:, t, :], ACT.Copy).then_inc(self.hi_done, 1)

    def dve_rest(self, nc, dve, g):
        for t in range(KT):
            dve.wait_ge(self.hi_done, g * KT + t + 1)
            nc.vector.tensor_tensor(self.lo[:, t, :], self.yf[:, t, :], f32(self.hi[:, t, :]), ALU.subtract
                                    ).then_inc(self.lo_done, 1)

    def split(self, eng, k, g):
        for t in range(KT):
            eng.wait_ge(self.full_done, g * KT + t + 1)
            eng.tensor_tensor(self.hi[:, t, :], self.yf[:, t, :], k.ones[:, :].to_broadcast([128, GT]), ALU.mult
                              ).then_inc(self.hi_done, 1)
        for t in range(KT):
            eng.wait_ge(self.hi_done, g * KT + t + 1)
            eng.tensor_tensor(self.lo[:, t, :], self.yf[:, t, :], f32(self.hi[:, t, :]), ALU.subtract
                              ).then_inc(self.lo_done, 1)


def mm3(nc, out, wh, wl, xh, xl, kt):
    for t in range(kt):
        nc.tensor.matmul(out, wh(t), xh(t), start=(t == 0), stop=False)
        nc.tensor.matmul(out, wh(t), xl(t), start=False, stop=False)
        ins = nc.tensor.matmul(out, wl(t), xh(t), start=False, stop=(t == kt - 1))
    return ins


def self_attention(nc, k, a, nxt):
    with ExitStack() as ctx:
        sb = lambda name, shape, dt=F32: ctx.enter_context(nc.sbuf_tensor("A_" + name, shape, dt))
        sem = phase_semaphores(k, 0)
        wh = [sb(f"w{w}_hi", [128, KT, INNER], F32R) for w in "qkv"]
        wl = [sb(f"w{w}_lo", [128, KT, INNER], F32R) for w in "qkv"]
        wo = sb("wo", [128, NP, D])
        gb_rows = sb("gain_shift_rows", [2 * KT, 128])
        first_gb = sb("gain_shift", [128, 2 * KT])
        ln = LN(nc, sb, sem, "", k.x, first_gb[:, 0:KT], first_gb[:, KT:2 * KT])
        q = sb("q", [128, NP, GT])
        kb = sb("k_blocks", [128, NP, GB, 2, N])
        v = sb("v", [N, GB, INNER])
        P = sb("probs", [N, 4, 2, N])
        PT = sb("probsT", [N, 4, 2, N])
        oT = sb("oT", [128, NP, N])
        nm = sb("neg_max", [N, 4, 2])
        sm = sb("sums", [N, 4, 2])
        rc = sb("rsums", [N, 4, 2])
        tmp = sb("attn_out", [N, D])
        SB, TB, OB = k.bank[0:2], k.bank[2:4], k.bank[4:6]
        PJ = k.bank[6:8]

        wo_in, w_hi, w_lo, wv_lo = sem("wo_in"), sem("w_hi"), sem("w_lo"), sem("wv_lo")
        kb_zero = sem("k_blocks_zeroed")
        gb_in, gb_turned, gb_set = sem("gain_shift_in"), sem("gain_shift_turned"), sem("gain_shift_set")
        init = sem("init")
        pj_done, pj_act, pj_dve = sem("proj_done"), sem("proj_out_act"), sem("proj_out_dve")
        s_done, max_done, exp_done = sem("scores_done"), sem("max_done"), sem("exp_done")
        rcp_done, norm_done, t_done = sem("rcp_done"), sem("norm_done"), sem("turned")
        pt_out, av_done, o_out = sem("probsT_out"), sem("av_done"), sem("oT_out")
        y_done, y_out, x_done = sem("y_done"), sem("y_out"), sem("x_done")
        SEQ0 = NP
        EXP0, NORM0, T0, PT0, AV0, O0, Y0 = 2 * 2, SEQ0, 4 + NP - LAG, 2 + NP - LAG, 4 + NP - LAG - 1, 2 + 1, 1
        QK, V = 2 * NP, 2 * GB
        UNITS = QK + V

        block = ctx.enter_context(nc.Block(no_gpsimd_drain=True))

        @block.sync
        def _(sp):
            xs = a["x"].rearrange("b n d -> n b d")
            sp.dma_start(k.x[:, 1:1 + GB, :], xs[:, 0:GB, :]).then_inc(k.x_in[0], 16)
            for i, name in enumerate(("L0_xattn_g1", "L0_xattn_b1")):
                sp.dma_start(gb_rows[KT * i:KT * (i + 1), :], a[name].rearrange("(c p) -> c p", p=128)
                             ).then_inc(gb_in, 16)
            for w, name in enumerate(("L0_xattn_Wq1", "L0_xattn_Wk1", "L0_xattn_Wv1")):
                sp.dma_start(k.stage[:, w, :].rearrange("p (t n) -> p t n", t=KT),
                             a[name].rearrange("(t p) n -> p t n", p=128)).then_inc(k.w_in[name], 16)
            sp.dma_start(k.x[:, 1 + GB:1 + B, :], xs[:, GB:B, :]).then_inc(k.x_in[1], 16)
            load_rows(sp, k, a)
            sp.dma_start(wo[:, :, :], a["L0_xattn_Wo1"].rearrange("(t p) n -> p t n", p=128)).then_inc(wo_in, 16)
            load_vectors(sp, k, a)
            sp.wait_ge(w_hi, 3)
            sp.wait_ge(w_lo, 2)
            sp.wait_ge(wv_lo, 1)
            nxt(sp)
            sp.wait_ge(ln.lo_done, (NG + 1) * KT)

        @block.gpsimd
        def _(pool):
            nc.gpsimd.memset(k.half[:, :], -0.5).then_inc(k.half_set, 1)
            nc.gpsimd.memset(k.eps[:, :], EPS).then_inc(k.half_set, 1)
            nc.gpsimd.memset(k.ones[:, :], 1.0).then_inc(k.half_set, 1)
            nc.gpsimd.memset(k.ident[:, :], 0.0).then_inc(k.ident_set, 1)
            pool.wait_ge(k.ident_set, 1)
            nc.gpsimd.affine_select(out=k.ident[:, :], in_=k.ident[:, :], compare_op=ALU.not_equal, fill=1.0, base=0,
                                    pattern=[[-1, 128]], channel_multiplier=1).then_inc(k.ident_set, 1)
            mask = k.vrows[0:1, :].rearrange("p (s t d) -> p s t d", s=4, t=2)
            for half in range(2):
                nc.gpsimd.memset(mask[:, :, half, :], -float(half)).then_inc(k.mask_set, 1)
            pool.wait_ge(k.ident_set, 2)
            pool.wait_ge(k.mask_set, 2)
            nc.gpsimd.memset(kb[64:128, :, :, 0, :].rearrange("p u b n -> p (u b) n"), 0.0).then_inc(kb_zero, 1)
            pool.wait_ge(kb_zero, 1)
            pool.wait_ge(k.half_set, 3)
            ln.pool_rstd(nc, pool, k, 0)
            nc.gpsimd.memset(k.x[:, 1 + B:1 + B + GB, :], 0.0).then_inc(k.pad_set, 1)
            nc.gpsimd.memset(k.x[:, 0, :], 0.0).then_inc(k.pad_set, 1)
            nc.gpsimd.memset(P[:, :, :, :], 0.0).then_inc(init, 1)
            nc.gpsimd.memset(PT[:, :, :, :], 0.0).then_inc(init, 1)
            nc.gpsimd.memset(v[:, GB - 1, :], 0.0).then_inc(init, 1)
            nc.gpsimd.memset(oT[:, :, :], 0.0).then_inc(init, 1)
            nc.gpsimd.memset(k.ctx_raw[:, :, :], 0.0).then_inc(k.ctx_cleared, 1)
            pool.wait_ge(w_hi, 3)
            nc.gpsimd.tensor_tensor(wl[2][:, :, :].rearrange("p t n -> p (t n)"), k.stage[:, 2, :],
                                    f32(wh[2][:, :, :]).rearrange("p t n -> p (t n)"), ALU.subtract).then_inc(wv_lo, 1)
            with pool.Fori(0, NG) as g:
                ln.pool_rstd(nc, pool, k, g + 1)
                ln.split(nc.gpsimd, k, g + 1)

        @block.scalar
        def _(act):
            for w in range(3):
                act.wait_ge(k.w_in[f"L0_xattn_W{'qkv'[w]}1"], 16)
                nc.scalar.activation(wh[w][:, :, :].rearrange("p t n -> p (t n)"), k.stage[:, w, :], ACT.Copy
                                     ).then_inc(w_hi, 1)
                if w == 0:
                    act.wait_ge(gb_turned, 1)
                    nc.scalar.activation(first_gb[:, :], k.bank[0][:, 0:2 * KT], ACT.Copy).then_inc(gb_set, 1)
                    act.wait_ge(gb_set, 1)
                    ln.act_full(nc, act, 0, PJ)
                    ln.act_round(nc, act, 0)
            act.sem_inc(exp_done, EXP0)
            act.sem_inc(o_out, O0)
            act.sem_inc(pt_out, PT0)

            def exps(t, u):
                act.wait_ge(max_done, t * NP + u + 1)
                act.wait_ge(t_done, (t + 1) * NP + u + 1)
                for j in range(2):
                    nc.scalar.activation(P[:, u % 4, j, :], SB[u % 2][0:N, j * N:(j + 1) * N], ACT.Exp,
                                         bias=nm[:, u % 4, j:j + 1],
                                         accum_out=sm[:, u % 4, j:j + 1]).then_inc(exp_done, 1)

            def pt_evac(t, u):
                act.wait_ge(t_done, 4 + (t + 1) * NP + u + 1)
                act.wait_ge(av_done, (t + 1) * NP + u + 1)
                nc.scalar.activation(PT[:, u % 4, :, :].rearrange("p j n -> p (j n)"), TB[u % 2][0:N, 0:2 * N],
                                     ACT.Copy).then_inc(pt_out, 1)

            def o_evac(t, h):
                act.wait_ge(av_done, 4 + (t + 1) * NP + 4 * h + 4)
                act.wait_ge(y_done, t + 1)
                nc.scalar.activation(oT[:, 4 * h:4 * h + 4, :].rearrange("p u n -> p (u n)"),
                                     OB[h][:, 0:4 * N], ACT.Copy).then_inc(o_out, 1)

            def late(t, i):
                if i < LAG:
                    pt_evac(t, NP - LAG + i)
                if i == LAG:
                    o_evac(t, 1)

            with act.Fori(0, NG) as g:
                for i in range(UNITS // 2):
                    act.wait_ge(pj_done, g * UNITS + 2 * i + 1)
                    if i < NP:
                        ins = nc.scalar.activation(q[:, i, :], PJ[0][:, 0:GT], ACT.Copy, scale=DH ** -0.5)
                    else:
                        ins = nc.scalar.activation(v[:, i - NP, 0:512], PJ[0][0:N, :], ACT.Copy)
                    ins.then_inc(pj_act, 1)
                    late(g * GB - 1, i)
                for b in range(GB):
                    t = g * GB + b
                    for u in range(NP):
                        if b == 0 and u == 2:
                            ln.act_full(nc, act, g + 1, PJ)
                        if u >= LAG:
                            pt_evac(t, u - LAG)
                        if b > 0:
                            late(t - 1, u)
                        exps(t, u)
                        if u == NP - 1:
                            o_evac(t, 0)
            for i in range(LAG + 1):
                late(B - 1, i)
            act.wait_ge(k.cols_turned, 1)
            nc.scalar.activation(k.consts[:, :], TB[0][:, 0:NCOL], ACT.Copy).then_inc(k.cols_set, 1)

        @block.vector
        def _(dve):
            dve.sem_inc(y_out, Y0)
            dve.sem_inc(norm_done, NORM0)
            nc.vector.memset(kb[0:64, :, :, 1, :].rearrange("p u b n -> p (u b) n"), 0.0).then_inc(init, 1)
            dve.wait_ge(k.x_in[0], 16)
            for b in range(GB):
                ln.dve_stats(nc, dve, 0, b)
            ln.dve_mean(nc, dve, 0, True)
            for b in range(GB):
                ln.dve_norm(nc, dve, 0, b, True)
            for w in range(2):
                dve.wait_ge(w_hi, w + 1)
                nc.vector.tensor_tensor(wl[w][:, :, :].rearrange("p t n -> p (t n)"), k.stage[:, w, :],
                                        f32(wh[w][:, :, :]).rearrange("p t n -> p (t n)"), ALU.subtract
                                        ).then_inc(w_lo, 1)
                if w == 0:
                    ln.dve_rest(nc, dve, 0)
            dve.wait_ge(init, 5)
            dve.wait_ge(k.pad_set, 2)

            def maxima(t, u):
                dve.wait_ge(s_done, t * NP + u + 1)
                nc.vector.tensor_reduce(nm[:, u % 4, :], SB[u % 2][0:N, 0:2 * N].rearrange("p (j n) -> p j n", j=2),
                                        AX.X, ALU.max, negate=True).then_inc(max_done, 1)

            def norm(t, u):
                dve.wait_ge(exp_done, EXP0 + t * 2 * NP + 2 * u + 2)
                nc.vector.reciprocal(rc[:, u % 4, :], sm[:, u % 4, :]).then_inc(rcp_done, 1)
                dve.wait_ge(rcp_done, t * NP + u + 1)
                nc.vector.tensor_tensor(P[:, u % 4, :, :], P[:, u % 4, :, :],
                                        rc[:, u % 4, :].unsqueeze(2).to_broadcast([N, 2, N]),
                                        ALU.mult).then_inc(norm_done, 1)

            def x_update(t, bank):
                dve.wait_ge(y_done, t + 2)
                dve.wait_ge(x_done, t + 1)
                nc.vector.tensor_tensor(tmp[:, :], bank[0:N, 0:D], k.bcast[:, 0, :], ALU.add).then_inc(y_out, 1)
                dve.wait_ge(y_out, Y0 + t + 2)
                xt = k.x[:, bass.ds(t + 1, 1), :].rearrange("p a d -> p (a d)")
                nc.vector.tensor_tensor(xt, xt, tmp[:, :], ALU.add).then_inc(x_done, 1)

            with dve.Fori(0, NG) as g:
                for i in range(UNITS // 2):
                    dve.wait_ge(pj_done, g * UNITS + 2 * i + 2)
                    if i < NP:
                        for j in range(2):
                            r = slice(64 * j, 64 * j + 64)
                            ins = nc.vector.tensor_copy(
                                kb[r, i, :, j, :], PJ[1][r, 0:GT].rearrange("p (b n) -> p b n", b=GB))
                            ins.then_inc(pj_dve, 1)
                    else:
                        nc.vector.tensor_copy(v[:, i - NP, 512:1024], PJ[1][0:N, :]).then_inc(pj_dve, 1)
                    if i == 1:
                        dve.wait_ge(k.x_in[1], 16)
                    if 0 < i <= GB:
                        ln.dve_stats(nc, dve, g + 1, i - 1)
                    if i == GB + 1:
                        ln.dve_mean(nc, dve, g + 1)
                    if i == 6:
                        dve.wait_ge(k.rows_in, ROW_LOADS)
                        x_update(g * GB - 1, SB[0])
                    if i >= 8:
                        ln.dve_norm(nc, dve, g + 1, i - 8)
                for b in range(GB):
                    t = g * GB + b
                    for u in range(NP):
                        maxima(t, u)
                        if u > 0:
                            norm(t, u - 1)
                        elif b > 0:
                            norm(t - 1, NP - 1)
                        if u == 2 and b > 1:
                            x_update(t - 2, PJ[0])
                x_update(g * GB + GB - 2, PJ[0])
                norm(g * GB + GB - 1, NP - 1)
            x_update(B - 1, SB[0])

        @block.tensor
        def _(pe):
            pe.wait_ge(k.ident_set, 2)
            pe.wait_ge(gb_in, 32)
            nc.tensor.transpose(k.bank[0][:, 0:2 * KT], gb_rows[:, :], k.ident[0:2 * KT, 0:2 * KT]
                                ).then_inc(gb_turned, 1)
            ln.pe_turn(nc, pe, k, 0, PJ)
            pe.wait_ge(gb_set, 1)
            pe.sem_inc(t_done, T0)
            pe.sem_inc(av_done, AV0)
            pe.wait_ge(w_lo, 1)
            pe.wait_ge(kb_zero, 1)
            pe.wait_ge(init, 5)

            def scores(b, t, u):
                pe.wait_ge(exp_done, t * 2 * NP + 2 * u + 2)
                nc.tensor.matmul(SB[u % 2][0:N, 0:2 * N], q[:, u, b * N:(b + 1) * N],
                                 kb[:, u, b, :, :].rearrange("p j n -> p (j n)"),
                                 start=True, stop=True).then_inc(s_done, 1)

            def turn(t, u):
                pe.wait_ge(norm_done, (t + 1) * NP + u + 1)
                pe.wait_ge(pt_out, (t + 1) * NP + u + 1)
                for j in range(2):
                    ins = nc.tensor.transpose(TB[u % 2][0:N, j * N:(j + 1) * N], P[:, u % 4, j, :], k.ident[0:N, 0:N])
                ins.then_inc(t_done, 1)

            def values(b, t, u):
                pe.wait_ge(pt_out, 2 + (t + 1) * NP + u + 1)
                if u % 4 == 0:
                    pe.wait_ge(o_out, (t + 1) * 2 + u // 4 + 1)
                for j in range(2):
                    h = 2 * u + j
                    ins = nc.tensor.matmul(OB[u // 4][64 * j:64 * j + 64, (u % 4) * N:(u % 4 + 1) * N],
                                           v[:, b, h * DH:(h + 1) * DH], PT[:, u % 4, j, :], start=True, stop=True)
                ins.then_inc(av_done, 1)

            def project(t, bank, part, parts):
                if part == 0:
                    pe.wait_ge(wo_in, 16)
                    pe.wait_ge(o_out, 2 + 2 * (t + 2))
                    pe.wait_ge(y_out, t + 2)
                n = NP // parts
                for u in range(part * n, part * n + n):
                    ins = nc.tensor.matmul(bank[0:N, 0:D], oT[:, u, :], wo[:, u, :], start=(u == 0), stop=(u == NP - 1))
                if part == parts - 1:
                    ins.then_inc(y_done, 1)

            def late(b, t, i, bank, parts):
                if i < LAG:
                    turn(t, NP - LAG + i)
                if i <= LAG:
                    values(b, t, NP - LAG - 1 + i)
                if LAG < i <= LAG + parts:
                    project(t, bank, i - LAG - 1, parts)

            with pe.Fori(0, NG) as g:
                pe.wait_ge(ln.lo_done, (g + 1) * KT)
                pe.wait_ge(y_out, g * GB + Y0)
                for i in range(UNITS):
                    if i >= 2 and i % 2 == 0:
                        pe.wait_ge(pj_act, g * (UNITS // 2) + i // 2)
                    if i >= 2 and i % 2 == 1:
                        pe.wait_ge(pj_dve, g * (2 * NP + GB) + min(i // 2, NP) * 2 + max(i // 2 - NP, 0))
                    if i == 1:
                        pe.wait_ge(w_lo, 2)
                    if i < QK:
                        w, m = i % 2, slice(128 * (i // 2), 128 * (i // 2 + 1))
                        ins = mm3(nc, PJ[i % 2][:, 0:GT], lambda t: wh[w][:, t, m], lambda t: wl[w][:, t, m],
                                  lambda t: ln.hi[:, t, :], lambda t: ln.lo[:, t, :], KT)
                    else:
                        if i == QK:
                            pe.wait_ge(wv_lo, 1)
                        b, n = (i - QK) // 2, slice(512 * (i % 2), 512 * (i % 2 + 1))
                        tok = slice(b * N, (b + 1) * N)
                        ins = mm3(nc, PJ[i % 2][0:N, :], lambda t: ln.hi[:, t, tok], lambda t: ln.lo[:, t, tok],
                                  lambda t: wh[2][:, t, n], lambda t: wl[2][:, t, n], KT)
                    ins.then_inc(pj_done, 1)
                    if i % 2 == 1:
                        late(GB - 1, g * GB - 1, i // 2, SB[0], 1)
                pe.wait_ge(y_out, g * GB + Y0 + 1)
                for b in range(GB):
                    t = g * GB + b
                    for u in range(NP):
                        scores(b, t, u)
                        if b == 0 and u == 1:
                            pe.wait_ge(pj_act, (g + 1) * (UNITS // 2))
                            pe.wait_ge(pj_dve, (g + 1) * (2 * NP + GB))
                            ln.pe_turn(nc, pe, k, g + 1, PJ)
                        if u >= LAG:
                            turn(t, u - LAG)
                        if u > LAG:
                            values(b, t, u - LAG - 1)
                        if b > 0:
                            if u == LAG + 1:
                                pe.wait_ge(ln.full_done, (g + 2) * KT)
                            late(b - 1, t - 1, u, PJ[0], 4)
            for i in range(LAG + 2):
                late(GB - 1, B - 1, i, SB[0], 1)
            pe.wait_ge(k.c_in, VECTOR_LOADS)
            pe.wait_ge(k.mask_set, 2)
            nc.tensor.transpose(TB[0][:, 0:NCOL], k.vrows[:, :], k.ident[0:NCOL, 0:NCOL]).then_inc(k.cols_turned, 1)


def context_weights_in(sp, stage, w, sem):
    n = w.shape[1]
    at = stage[:, 0:2 * n].rearrange("p (t n) -> p t n", t=2)
    sp.dma_start(at[:, 0, :], w[0:128, :]).then_inc(sem, 16)
    sp.dma_start(at[0:CR, 1, :], w[128:C, :]).then_inc(sem, 16)
    sp.dma_start(at[CR:128, 1, :], w[128:C, :]).then_inc(sem, 16)


CONTEXT_LOADS = 3 * 16


def mm5(nc, out, lh, rh, turned):
    (w, wl), (c0, c0l, c1) = (rh, lh) if turned else (lh, rh)
    passes = [(w[0], c0), (w[0], c0l), (wl[0], c0), (w[1], c1), (wl[1], c1)]
    for i, (x, y) in enumerate(passes):
        ins = nc.tensor.matmul(out, y if turned else x, x if turned else y, start=(i == 0), stop=(i == 4))
    return ins


def load_context(sp, raw, c, t, sem):
    src = c[bass.ds(t, 1), :, :].rearrange("a s c -> (a s) c")
    sp.dma_start(raw[:, 0:NS - 1, :], src[0:ST * (NS - 1), :].rearrange("(n p) c -> p n c", p=ST)).then_inc(sem, 16)
    sp.dma_start(raw[0:S - ST * (NS - 1), NS - 1, :], src[ST * (NS - 1):S, :]).then_inc(sem, 16)


class Context:

    def __init__(self, sb, sem, raw, first_in):
        self.raw, self.first_in = raw, first_in
        self.T = sb("ctxT", [128, 3, SP], F32R)
        self.loaded = sem("ctx_loaded")
        self.turned = sem("ctx_turned")
        self.hi_done = sem("ctx_hi_done")
        self.lo_done = sem("ctx_lo_done")

    LOADS = 32

    def load(self, sp, c, t):
        load_context(sp, self.raw, c, t, self.loaded)

    def sp_loop(self, sp, c):
        with sp.Fori(1, B) as t:
            sp.wait_ge(self.turned, t)
            self.load(sp, c, t)
        sp.wait_ge(self.turned, B)
        self.load(sp, c, 0)
        sp.wait_ge(self.turned, B + 1)

    def pe_turn(self, nc, pe, k, t, banks):
        if isinstance(t, int):
            pe.wait_ge(self.first_in, self.LOADS)
        else:
            pe.wait_ge(self.loaded, t * self.LOADS)
        for s in range(NS):
            cols = slice(ST * s, ST * (s + 1))
            nc.tensor.transpose(banks[0][:, cols], self.raw[:, s, 0:128], k.ident[0:ST, 0:ST])
            ins = nc.tensor.transpose(banks[1][0:CR, cols], self.raw[:, s, 128:C], k.ident[0:ST, 0:ST])
        ins.then_inc(self.turned, 1)

    def act_hi(self, nc, act, t, banks):
        act.wait_ge(self.turned, t + 1)
        nc.scalar.activation(self.T[:, 0, :], banks[0][:, 0:SP], ACT.Copy).then_inc(self.hi_done, 1)
        nc.scalar.activation(self.T[0:CR, 2, :], banks[1][0:CR, 0:SP], ACT.Copy).then_inc(self.hi_done, 1)

    def dve_lo(self, nc, dve, t, banks):
        dve.wait_ge(self.hi_done, 2 * (t + 1))
        nc.vector.tensor_tensor(self.T[:, 1, :], banks[0][:, 0:SP], f32(self.T[:, 0, :]), ALU.subtract
                                ).then_inc(self.lo_done, 1)
        nc.vector.tensor_tensor(self.T[CR:128, 2, :], banks[1][0:CR, 0:SP], f32(self.T[0:CR, 2, :]), ALU.subtract
                                ).then_inc(self.lo_done, 1)

    def cols(self, at):
        return [self.T[:, i, at] for i in range(3)]


def cross_attention(nc, k, a, nxt):
    with ExitStack() as ctx:
        sb = lambda name, shape, dt=F32: ctx.enter_context(nc.sbuf_tensor("B_" + name, shape, dt))
        sem = phase_semaphores(k, 1)
        wqh, wkh, wvh = [sb(f"w{w}_hi", [128, 2, INNER], F32R) for w in "qkv"]
        wql, wkl, wvl = [sb(f"w{w}_lo", [128, 2, INNER], F32R) for w in "qkv"]
        wo = sb("wo", [128, NP, D])
        ln = LN(nc, sb, sem, "", k.x, k.consts[:, 5:7], k.consts[:, 7:9])
        cx = Context(sb, sem, k.ctx_raw, k.first_ctx_in[0])
        qg = sb("q_group", [128, NP, GT])
        qh = sb("q_hi", [128, NP, N], F32R)
        ql = sb("q_lo", [128, NP, N], F32R)
        kh = sb("k_hi", [128, NP, SP], F32R)
        kl = sb("k_lo", [128, NP, SP], F32R)
        v = sb("v", [ST, NS, INNER])
        P = sb("probs", [N, PS, 2, SP])
        PT = sb("probsT", [ST, 2, 2, NS, N])
        oT = sb("oT", [128, NP, N])
        nm = sb("neg_max", [N, PS, 2])
        sm = sb("sums", [N, PS, 2])
        rc = sb("rsums", [N, PS, 2])
        tmp = sb("attn_out", [N, D])
        SB, TB, OB, YB, PJ = k.bank[0:2], k.bank[2:4], k.bank[4], k.bank[5], k.bank[6:8]

        wo_in, w_hi, w_lo, wv_lo, init = sem("wo_in"), sem("w_hi"), sem("w_lo"), sem("wv_lo"), sem("init")
        q_mm, q_act, q_dve, qh_done, ql_done = sem("q_mm"), sem("q_act"), sem("q_dve"), sem("qh"), sem("ql")
        k_mm, k_hi, k_lo = sem("k_mm"), sem("k_hi_done"), sem("k_lo_done")
        v_mm, v_out = sem("v_mm"), sem("v_out")
        s_done, max_done, exp_done = sem("scores_done"), sem("max_done"), sem("exp_done")
        rcp_done, norm_done, t_done = sem("rcp_done"), sem("norm_done"), sem("turned")
        pt_act, pt_dve, av_done, o_out = sem("probsT_act"), sem("probsT_dve"), sem("av_done"), sem("oT_out")
        y_half, y_done, y_out, x_done = sem("y_half_done"), sem("y_done"), sem("y_out"), sem("x_done")
        EXP0, NORM0, T0, PT0, AV0, O0, Y0 = 2, NP - 1, PS + NP - LAG, 1 + NP - LAG, 2 + NP - LAG - 1, 1 + 1, 1

        block = ctx.enter_context(nc.Block(no_gpsimd_drain=True))

        @block.sync
        def _(sp):
            sp.dma_start(wo[:, :, :], a["L0_xattn_Wo2"].rearrange("(t p) n -> p t n", p=128)).then_inc(wo_in, 16)
            sp.wait_ge(w_hi, 3)
            sp.wait_ge(w_lo, 2)
            sp.wait_ge(wv_lo, 3)
            nxt(sp)
            clear_semaphores(sp, k, 0)
            cx.sp_loop(sp, a["ctx_768"])
            sp.wait_ge(ln.lo_done, (NG + 1) * KT)

        @block.gpsimd
        def _(pool):
            ln.pool_rstd(nc, pool, k, 0)
            nc.gpsimd.memset(P[:, :, :, :], 0.0).then_inc(init, 1)
            nc.gpsimd.memset(PT[:, :, :, :, :].rearrange("p r j s n -> p (r j s n)"), 0.0).then_inc(init, 1)
            nc.gpsimd.memset(oT[:, :, :], 0.0).then_inc(init, 1)
            nc.gpsimd.memset(v[:, :, :], 0.0).then_inc(wv_lo, 1)
            pool.wait_ge(wv_lo, 1)
            pool.wait_ge(w_hi, 3)
            raw = k.stage[:, 2, :].rearrange("p (t n) -> p t n", t=2)
            nc.gpsimd.tensor_tensor(wvl[:, 0, :], raw[:, 0, :], f32(wvh[:, 0, :]), ALU.subtract).then_inc(wv_lo, 1)
            pool.wait_ge(wv_lo, 2)
            nc.gpsimd.tensor_tensor(wvl[0:CR, 1, :], raw[0:CR, 1, :], f32(wvh[0:CR, 1, :]), ALU.subtract
                                    ).then_inc(wv_lo, 1)
            with pool.Fori(0, NG) as g:
                ln.pool_rstd(nc, pool, k, g + 1)
                for b in range(GB):
                    t = g * GB + b
                    pool.wait_ge(q_act, (g + 1) * (NP // 2))
                    pool.wait_ge(q_dve, (g + 1) * (NP // 2))
                    for u in range(NP):
                        pool.wait_ge(s_done, 2 * (t * NP + u + 1))
                        nc.gpsimd.tensor_tensor(qh[:, u, :], qg[:, u, b * N:(b + 1) * N],
                                                k.ones[:, :].to_broadcast([128, N]), ALU.mult
                                                ).then_inc(qh_done, 1)
                        pool.wait_ge(qh_done, t * NP + u + 1)
                        nc.gpsimd.tensor_tensor(ql[:, u, :], qg[:, u, b * N:(b + 1) * N], f32(qh[:, u, :]),
                                                ALU.subtract).then_inc(ql_done, 1)
                ln.split(nc.gpsimd, k, g + 1)

        @block.scalar
        def _(act):
            cx.act_hi(nc, act, 0, k.bank[2:4])
            for i, (w, src) in enumerate(((wkh, 1), (wqh, 0), (wvh, 2))):
                act.wait_ge(k.w_in[f"L0_xattn_W{'qkv'[src]}2"], 16 if src == 0 else CONTEXT_LOADS)
                nc.scalar.activation(w[:, :, :].rearrange("p t n -> p (t n)"), k.stage[:, src, :], ACT.Copy
                                     ).then_inc(w_hi, 1)
                if i == 1:
                    ln.act_full(nc, act, 0, PJ)
                    ln.act_round(nc, act, 0)
            act.sem_inc(o_out, O0)
            act.sem_inc(exp_done, EXP0)
            act.sem_inc(pt_act, PT0)

            def exps(t, u):
                act.wait_ge(t_done, (t + 1) * NP + u + 1)
                for j in range(2):
                    act.wait_ge(max_done, 2 * (t * NP + u) + j + 1)
                    nc.scalar.activation(P[:, u % PS, j, 0:S], SB[j][0:N, 0:S], ACT.Exp, bias=nm[:, u % PS, j:j + 1],
                                         accum_out=sm[:, u % PS, j:j + 1]).then_inc(exp_done, 1)

            def pt_evac(t, u):
                act.wait_ge(t_done, PS + (t + 1) * NP + u + 1)
                act.wait_ge(av_done, (t + 1) * NP + u + 1)
                nc.scalar.activation(PT[:, u % 2, 0, :, :].rearrange("p s n -> p (s n)"), TB[0][0:ST, 0:NS * N],
                                     ACT.Copy).then_inc(pt_act, 1)

            def o_evac(t, h):
                act.wait_ge(av_done, 2 + (t + 1) * NP + 4 * h + 4)
                act.wait_ge(y_done if h else y_half, t + 1)
                nc.scalar.activation(oT[:, 4 * h:4 * h + 4, :].rearrange("p u n -> p (u n)"),
                                     OB[:, 0:4 * N], ACT.Copy).then_inc(o_out, 1)

            def keys(t, u, bank):
                act.wait_ge(k_mm, t * NP + u + 1)
                nc.scalar.activation(kh[:, u, :], bank[:, 0:SP], ACT.Copy).then_inc(k_hi, 1)

            for u in range(2):
                keys(0, u, PJ[u])
            with act.Fori(0, NG) as g:
                for i in range(NP // 2):
                    act.wait_ge(q_mm, g * NP + 2 * i + 1)
                    act.wait_ge(ql_done, g * GB * NP)
                    nc.scalar.activation(qg[:, 2 * i, :], PJ[0][:, 0:GT], ACT.Copy, scale=DH ** -0.5
                                         ).then_inc(q_act, 1)
                ln.act_full(nc, act, g + 1, PJ)
                with act.Fori(0, GB) as b:
                    t = g * GB + b
                    for u in range(NP):
                        pt_evac(t if u >= LAG else t - 1, (u - LAG) % NP)
                        if u == LAG:
                            o_evac(t - 1, 1)
                        if u == NP - 1:
                            o_evac(t, 0)
                        if u == NP - 2:
                            cx.act_hi(nc, act, t + 1, PJ)
                        exps(t, u)
                        if u < NP - 2:
                            keys(t, u + 2, PJ[0])
                            act.wait_ge(v_mm, t * 2 * NS + u + 1)
                            h = u // NS
                            nc.scalar.activation(v[:, u % NS, 512 * h:512 * (h + 1)], PJ[1][0:ST, :], ACT.Copy
                                                 ).then_inc(v_out, 1)
                        if u == NP - 1:
                            for w in range(2):
                                keys(t + 1, w, PJ[w])
            for u in range(NP - LAG, NP):
                pt_evac(B - 1, u)
            o_evac(B - 1, 1)

        @block.vector
        def _(dve):
            dve.sem_inc(y_out, Y0)
            dve.sem_inc(norm_done, NORM0)
            dve.sem_inc(pt_dve, PT0)
            for b in range(GB):
                ln.dve_stats(nc, dve, 0, b)
            ln.dve_mean(nc, dve, 0, True)
            cx.dve_lo(nc, dve, 0, k.bank[2:4])
            nc.vector.memset(f32(wkl[CR:128, 1, :]), 0.0).then_inc(init, 1)
            dve.wait_ge(w_hi, 1)
            raw = k.stage[:, 1, :].rearrange("p (t n) -> p t n", t=2)
            nc.vector.tensor_tensor(wkl[:, 0, :], raw[:, 0, :], f32(wkh[:, 0, :]), ALU.subtract)
            nc.vector.tensor_tensor(wkl[0:CR, 1, :], raw[0:CR, 1, :], f32(wkh[0:CR, 1, :]), ALU.subtract
                                    ).then_inc(w_lo, 1)
            for b in range(GB):
                ln.dve_norm(nc, dve, 0, b, True)
            dve.wait_ge(w_hi, 2)
            nc.vector.tensor_tensor(wql[:, :, :].rearrange("p t n -> p (t n)"), k.stage[:, 0, :],
                                    f32(wqh[:, :, :]).rearrange("p t n -> p (t n)"), ALU.subtract).then_inc(w_lo, 1)
            ln.dve_rest(nc, dve, 0)
            nc.vector.memset(f32(wvl[CR:128, 1, :]), 0.0).then_inc(init, 1)
            nc.vector.memset(OB[:, 0:4 * N], 0.0).then_inc(init, 1)
            nc.vector.memset(sm[:, PS - 1, :], 1.0).then_inc(init, 1)
            dve.wait_ge(init, 7)

            def maxima(t, u):
                for j in range(2):
                    dve.wait_ge(s_done, 2 * (NP + t * NP + u) + j + 1)
                    nc.vector.tensor_reduce(nm[:, u % PS, j:j + 1], SB[j][0:N, 0:S], AX.X, ALU.max, negate=True
                                            ).then_inc(max_done, 1)

            def norm(t, u):
                dve.wait_ge(exp_done, EXP0 + t * 2 * NP + 2 * u + 2)
                nc.vector.reciprocal(rc[:, u % PS, :], sm[:, u % PS, :]).then_inc(rcp_done, 1)
                dve.wait_ge(rcp_done, t * NP + u + 2)
                for j in range(2):
                    ins = nc.vector.tensor_scalar(P[:, u % PS, j, 0:S], P[:, u % PS, j, 0:S],
                                                  rc[:, u % PS, j:j + 1], None, ALU.mult)
                ins.then_inc(norm_done, 1)

            def pt_evac(t, u):
                dve.wait_ge(t_done, PS + (t + 1) * NP + u + 1)
                dve.wait_ge(av_done, (t + 1) * NP + u + 1)
                nc.vector.tensor_copy(PT[:, u % 2, 1, :, :].rearrange("p s n -> p (s n)"), TB[1][0:ST, 0:NS * N]
                                      ).then_inc(pt_dve, 1)

            def keys(t, u, bank):
                dve.wait_ge(k_hi, t * NP + u + 1)
                nc.vector.tensor_tensor(kl[:, u, :], bank[:, 0:SP], f32(kh[:, u, :]), ALU.subtract).then_inc(k_lo, 1)

            def x_update(t):
                dve.wait_ge(y_done, t + 2)
                dve.wait_ge(x_done, t + 1)
                nc.vector.tensor_tensor(tmp[:, :], YB[0:N, 0:D], k.bcast[:, 1, :], ALU.add).then_inc(y_out, 1)
                dve.wait_ge(y_out, Y0 + t + 2)
                xt = k.x[:, bass.ds(t + 1, 1), :].rearrange("p a d -> p (a d)")
                nc.vector.tensor_tensor(xt, xt, tmp[:, :], ALU.add).then_inc(x_done, 1)

            for u in range(2):
                keys(0, u, PJ[u])
            with dve.Fori(0, NG) as g:
                for b in range(GB):
                    ln.dve_stats(nc, dve, g + 1, b)
                ln.dve_mean(nc, dve, g + 1)
                for i in range(NP // 2):
                    dve.wait_ge(q_mm, g * NP + 2 * i + 2)
                    dve.wait_ge(ql_done, g * GB * NP)
                    nc.vector.tensor_scalar(qg[:, 2 * i + 1, :], PJ[1][:, 0:GT], DH ** -0.5, None, ALU.mult
                                            ).then_inc(q_dve, 1)
                    ln.dve_norm(nc, dve, g + 1, i)
                with dve.Fori(0, GB) as b:
                    t = g * GB + b
                    for u in range(NP):
                        pt_evac(t if u >= LAG else t - 1, (u - LAG) % NP)
                        maxima(t, u)
                        norm(t if u else t - 1, (u - 1) % NP)
                        if u < NP - 2:
                            keys(t, u + 2, PJ[0])
                        if u == NP - 2:
                            cx.dve_lo(nc, dve, t + 1, PJ)
                        if u == NP - 1:
                            for w in range(2):
                                keys(t + 1, w, PJ[w])
                            x_update(t - 1)
            norm(B - 1, NP - 1)
            for u in range(NP - LAG, NP):
                pt_evac(B - 1, u)
            x_update(B - 1)

        @block.tensor
        def _(pe):
            cx.pe_turn(nc, pe, k, 0, k.bank[2:4])
            ln.pe_turn(nc, pe, k, 0, PJ)
            pe.sem_inc(t_done, T0)
            pe.sem_inc(av_done, AV0)
            pe.sem_inc(s_done, 2 * NP)
            pe.wait_ge(w_lo, 1)
            pe.wait_ge(cx.lo_done, 2)

            def keys(t, u, bank):
                m = slice(128 * u, 128 * (u + 1))
                mm5(nc, bank[:, 0:SP], ([wkh[:, i, m] for i in range(2)], [wkl[:, i, m] for i in range(2)]),
                    cx.cols(slice(0, SP)), False).then_inc(k_mm, 1)

            def new_values(t, u):
                h, s = u // NS, u % NS
                n = slice(512 * h, 512 * (h + 1))
                mm5(nc, PJ[1][0:ST, :], cx.cols(slice(ST * s, ST * (s + 1))),
                    ([wvh[:, i, n] for i in range(2)], [wvl[:, i, n] for i in range(2)]), True).then_inc(v_mm, 1)

            def scores(t, u):
                pe.wait_ge(ql_done, t * NP + u + 1)
                pe.wait_ge(k_lo, t * NP + u + 1)
                for i, (x, y) in enumerate(((qh, kh), (qh, kl), (ql, kh))):
                    for j in range(2):
                        if i == 0:
                            pe.wait_ge(exp_done, 2 * (t * NP + u) + j + 1)
                        r = slice(64 * j, 64 * j + 64)
                        ins = nc.tensor.matmul(SB[j][0:N, 0:SP], x[r, u, :], y[r, u, :], start=(i == 0), stop=(i == 2))
                        if i == 2:
                            ins.then_inc(s_done, 1)

            def turn(t, u):
                pe.wait_ge(norm_done, (t + 1) * NP + u + 1)
                pe.wait_ge(pt_act, (t + 1) * NP + u + 1)
                pe.wait_ge(pt_dve, (t + 1) * NP + u + 1)
                for j in range(2):
                    for s in range(NS):
                        ins = nc.tensor.transpose(TB[j][0:ST, s * N:(s + 1) * N],
                                                  P[:, u % PS, j, ST * s:ST * (s + 1)], k.ident[0:N, 0:N])
                ins.then_inc(t_done, 1)

            def values(t, u):
                pe.wait_ge(pt_act, 1 + (t + 1) * NP + u + 1)
                pe.wait_ge(pt_dve, 1 + (t + 1) * NP + u + 1)
                if u % 4 == 0:
                    pe.wait_ge(o_out, (t + 1) * 2 + u // 4 + 1)
                    if u == 0:
                        pe.wait_ge(v_out, (t + 1) * 2 * NS - NS)
                    elif not isinstance(t, int):
                        pe.wait_ge(v_out, (t + 1) * 2 * NS)
                for s in range(NS):
                    for j in range(2):
                        h = 2 * u + j
                        ins = nc.tensor.matmul(OB[64 * j:64 * j + 64, (u % 4) * N:(u % 4 + 1) * N],
                                               v[:, s, h * DH:(h + 1) * DH], PT[:, u % 2, j, s, :],
                                               start=(s == 0), stop=(s == NS - 1))
                ins.then_inc(av_done, 1)

            def project(t, part):
                if part == 0:
                    pe.wait_ge(o_out, 1 + 2 * (t + 2))
                    pe.wait_ge(y_out, t + 2)
                for u in range(2 * part, 2 * part + 2):
                    ins = nc.tensor.matmul(YB[0:N, 0:D], oT[:, u, :], wo[:, u, :], start=(u == 0), stop=(u == NP - 1))
                if part % 2:
                    ins.then_inc((y_half, y_done)[part // 2], 1)

            pe.wait_ge(ln.full_done, KT)
            for u in range(2):
                keys(0, u, PJ[u])
            pe.wait_ge(w_lo, 2)
            pe.wait_ge(init, 7)
            pe.wait_ge(wo_in, 16)
            with pe.Fori(0, NG) as g:
                pe.wait_ge(ln.lo_done, (g + 1) * KT)
                for i in range(NP):
                    if i < 2:
                        pe.wait_ge(k_lo, g * GB * NP + i + 1)
                    if i >= 2:
                        pe.wait_ge((q_act, q_dve)[i % 2], g * (NP // 2) + i // 2)
                    m = slice(128 * i, 128 * (i + 1))
                    mm3(nc, PJ[i % 2][:, 0:GT], lambda t: wqh[:, t, m], lambda t: wql[:, t, m],
                        lambda t: ln.hi[:, t, :], lambda t: ln.lo[:, t, :], KT).then_inc(q_mm, 1)
                pe.wait_ge(q_act, (g + 1) * (NP // 2))
                pe.wait_ge(q_dve, (g + 1) * (NP // 2))
                ln.pe_turn(nc, pe, k, g + 1, PJ)
                pe.wait_ge(wv_lo, 3)
                with pe.Fori(0, GB) as b:
                    t = g * GB + b
                    for u in range(NP):
                        turn(t if u >= LAG else t - 1, (u - LAG) % NP)
                        values(t if u > LAG else t - 1, (u - LAG - 1) % NP)
                        if u == NP - 2:
                            pe.wait_ge(k_lo, t * NP + NP)
                            pe.wait_ge(v_out, (t + 1) * 2 * NS)
                            cx.pe_turn(nc, pe, k, t + 1, PJ)
                        scores(t, u)
                        if u == 0:
                            pe.wait_ge(ln.full_done, (g + 2) * KT)
                        if u < NP - 2:
                            pe.wait_ge(k_lo, t * NP + (1 if u == 0 else u + 2))
                            keys(t, u + 2, PJ[0])
                            if u == 0:
                                pe.wait_ge(k_lo, t * NP + 2)
                            else:
                                pe.wait_ge(v_out, t * 2 * NS + u)
                            new_values(t, u)
                        if u == NP - 1:
                            pe.wait_ge(cx.lo_done, 2 * (t + 2))
                            for w in range(2):
                                keys(t + 1, w, PJ[w])
                        if LAG < u <= LAG + 4:
                            project(t - 1, u - LAG - 1)
            for i in range(LAG + 1):
                if i < LAG:
                    turn(B - 1, NP - LAG + i)
                values(B - 1, NP - LAG - 1 + i)
            for part in range(4):
                project(B - 1, part)


def feed_forward(nc, k, a, nxt, p, gated, load_out, wp_raw, wf_raw, wp_name, wf_name, cols, src, gain, shift):
    with ExitStack() as ctx:
        sb = lambda name, shape, dt=F32: ctx.enter_context(nc.sbuf_tensor(p + name, shape, dt))
        sem = phase_semaphores(k, 0)
        HT = FF // 128
        NW = 2 * FF if gated else FF
        bp, bf = k.consts[:, cols[0]:cols[0] + NW // 128], k.consts[:, cols[1]:cols[1] + KT]
        wph, wpl = sb("wp_hi", [128, KT, NW], F32R), sb("wp_lo", [128, KT, NW], F32R)
        wfh, wfl = sb("wf_hi", [128, HT, D], F32R), sb("wf_lo", [128, HT, D], F32R)
        ln = LN(nc, sb, sem, "", src, gain, shift)
        hi, lo = [[b, sb("xT_odd" + n, [128, KT, GT], F32R)] for b, n in ((ln.hi, "_hi"), (ln.lo, "_lo"))]
        gl = sb("gelu", [128, 2, GT])
        ph = sb("hidden_hi", [128, 2, GT], F32R)
        pl = sb("hidden_lo", [128, 2, GT], F32R)
        pf = sb("hidden", [128, 2, GT]) if gated else gl
        yT = sb("yT", [128, KT, GT])
        AB, GBK, YB, TB = k.bank[0:2], k.bank[2:4], k.bank[4:6], k.bank[6:8]
        w_hi, w_lo, wf_hi, wf_lo = sem("w_hi"), sem("w_lo"), sem("wf_hi"), sem("wf_lo")
        a_mm, g_mm, y_mm = sem("value_mm"), sem("gate_mm"), sem("y_mm")
        gelu_done, h_done, hh_done, hl_done = sem("gelu_done"), sem("hidden_done"), sem("hidden_hi"), sem("hidden_lo")
        yT_done, y_turned, x_done = sem("yT_done"), sem("y_turned"), sem("x_done")
        QW = 4
        parts = []
        for i in range(QW // 2):
            for half in ((0, 1) if gated else (0,)):
                w = FF // (QW // 2)
                parts.append(slice(half * FF + i * w, half * FF + (i + 1) * w))

        block = ctx.enter_context(nc.Block(no_gpsimd_drain=True))

        @block.sync
        def _(sp):
            sp.wait_ge(w_hi, len(parts))
            sp.wait_ge(w_lo, len(parts))
            sp.wait_ge(wf_hi, 1)
            sp.wait_ge(wf_lo, 1)
            nxt(sp)
            clear_semaphores(sp, k, 1)
            if load_out is not None:
                ov = load_out.rearrange("b n d -> n b d")
                with sp.Fori(0, NG) as g:
                    sp.wait_ge(x_done, 2 * (g + 1))
                    sp.dma_start(ov[:, bass.ds(g * GB, GB), :], k.x[:, bass.ds(g * GB + 1, GB), :]
                                 ).then_inc(k.out_done, 16)
                sp.wait_ge(k.out_done, NG * 16)

        @block.gpsimd
        def _(pool):
            ln.pool_rstd(nc, pool, k, 0)
            with pool.Fori(0, NG) as g:
                ln.pool_rstd(nc, pool, k, g + 1)

        @block.scalar
        def _(act):
            act.wait_ge(k.w_in[wp_name], 16)
            for i, c in enumerate(parts):
                nc.scalar.activation(wph[:, :, c], wp_raw[:, :, c], ACT.Copy).then_inc(w_hi, 1)
                if i == (1 if gated else 0):
                    ln.act_full(nc, act, 0, TB)
                    ln.act_round(nc, act, 0)
            act.wait_ge(k.w_in[wf_name], 16)
            nc.scalar.activation(wfh[:, :, :], wf_raw, ACT.Copy).then_inc(wf_hi, 1)

            def hidden(g, j):
                act.wait_ge(g_mm, g * HT + j + 1)
                if not (isinstance(g, int) and j == 0):
                    act.wait_ge(h_done if gated else hl_done, g * HT + j - 1)
                nc.scalar.activation(gl[:, j % 2, :], GBK[j % 2][:, 0:GT], ACT.Gelu,
                                     bias=bp[:, NW // 128 - HT + j:NW // 128 - HT + j + 1]).then_inc(gelu_done, 1)

            def round_hidden(g, j):
                act.wait_ge(y_mm, g * HT + j - 1 if j > 1 else g * HT)
                act.wait_ge(h_done if gated else gelu_done, g * HT + j + 1)
                nc.scalar.activation(ph[:, j % 2, :], pf[:, j % 2, :], ACT.Copy).then_inc(hh_done, 1)

            hidden(0, 0)
            with act.Fori(0, NG // 2) as pair:
                for odd in range(2):
                    g = 2 * pair + odd
                    for j in range(HT):
                        round_hidden(g, j)
                        if j < HT - 1:
                            hidden(g, j + 1)
                        else:
                            hidden(g + 1, 0)
                        if j == HT // 2 + 1:
                            ln.act_full(nc, act, g + 1, TB)
                        if j == HT // 2 + 2:
                            for t in range(KT):
                                act.wait_ge(ln.full_done, (g + 1) * KT + t + 1)
                                act.wait_ge(g_mm, g * HT)
                                nc.scalar.activation(hi[1 - odd][:, t, :], ln.yf[:, t, :], ACT.Copy
                                                     ).then_inc(ln.hi_done, 1)
                    act.wait_ge(y_mm, (g + 1) * HT)
                    for m in range(KT):
                        act.wait_ge(y_turned, g * GB)
                        nc.scalar.activation(yT[:, m, :], YB[m][:, 0:GT], ACT.Identity, bias=bf[:, m:m + 1]
                                             ).then_inc(yT_done, 1)

        @block.vector
        def _(dve):
            for b in range(GB):
                ln.dve_stats(nc, dve, 0, b)
            ln.dve_mean(nc, dve, 0, True)
            for i, c in enumerate(parts):
                dve.wait_ge(w_hi, i + 1)
                nc.vector.tensor_tensor(wpl[:, :, c], wp_raw[:, :, c], f32(wph[:, :, c]), ALU.subtract).then_inc(w_lo, 1)
                if i == 0:
                    for b in range(GB):
                        ln.dve_norm(nc, dve, 0, b, True)
                if i == (1 if gated else 0):
                    ln.dve_rest(nc, dve, 0)
            dve.wait_ge(wf_hi, 1)
            nc.vector.tensor_tensor(wfl[:, :, :], wf_raw, f32(wfh[:, :, :]), ALU.subtract).then_inc(wf_lo, 1)

            def hidden(g, j):
                if not gated:
                    return
                dve.wait_ge(gelu_done, g * HT + j + 1)
                if not (isinstance(g, int) and j == 0):
                    dve.wait_ge(hl_done, g * HT + j - 1)
                nc.vector.scalar_tensor_tensor(pf[:, j % 2, :], AB[j % 2][:, 0:GT], bp[:, j:j + 1], gl[:, j % 2, :],
                                               ALU.add, ALU.mult).then_inc(h_done, 1)

            def rest(g, j):
                dve.wait_ge(hh_done, g * HT + j + 1)
                nc.vector.tensor_tensor(pl[:, j % 2, :], pf[:, j % 2, :], f32(ph[:, j % 2, :]), ALU.subtract
                                        ).then_inc(hl_done, 1)

            hidden(0, 0)
            with dve.Fori(0, NG // 2) as pair:
                for odd in range(2):
                    g = 2 * pair + odd
                    for j in range(HT):
                        rest(g, j)
                        if j < HT - 1:
                            hidden(g, j + 1)
                        else:
                            hidden(g + 1, 0)
                        if j < 2:
                            ln.dve_stats(nc, dve, g + 1, 2 * j)
                            ln.dve_stats(nc, dve, g + 1, 2 * j + 1)
                        if j == 1:
                            ln.dve_mean(nc, dve, g + 1)
                        if j in (2, 3):
                            for b in range(2 * j - 4, 2 * j - 2):
                                ln.dve_norm(nc, dve, g + 1, b)
                        if j == HT // 2 + 2:
                            for t in range(KT):
                                dve.wait_ge(ln.hi_done, (g + 1) * KT + t + 1)
                                nc.vector.tensor_tensor(lo[1 - odd][:, t, :], ln.yf[:, t, :],
                                                        f32(hi[1 - odd][:, t, :]), ALU.subtract
                                                        ).then_inc(ln.lo_done, 1)
                    for i in range(GB // 2):
                        dve.wait_ge(y_turned, g * GB + 2 * i + 2)
                        xt = k.x[:, bass.ds(g * GB + 2 * i + 1, 2), :].rearrange("p a d -> p (a d)")
                        nc.vector.tensor_tensor(xt, xt, TB[i][0:N, :], ALU.add).then_inc(x_done, 1)

        @block.tensor
        def _(pe):
            ln.pe_turn(nc, pe, k, 0, TB)
            pe.wait_ge(ln.lo_done, KT)

            def product(g, j, odd):
                first = isinstance(g, int) and j == 0
                for bank, at, used, done in ((AB, 128 * j, h_done, a_mm), (GBK, NW - FF + 128 * j, gelu_done, g_mm)):
                    if done is a_mm and not gated:
                        continue
                    if not first:
                        pe.wait_ge(used, g * HT + j - 1)
                    m = slice(at, at + 128)
                    mm3(nc, bank[j % 2][:, 0:GT], lambda t: wph[:, t, m], lambda t: wpl[:, t, m],
                        lambda t: hi[odd][:, t, :], lambda t: lo[odd][:, t, :], KT).then_inc(done, 1)

            def output(g, j):
                pe.wait_ge(hl_done, g * HT + j + 1)
                if j == 0:
                    pe.wait_ge(yT_done, g * KT)
                for m in range(KT):
                    c = slice(128 * m, 128 * (m + 1))
                    for i, (w, h) in enumerate(((wfh, ph), (wfh, pl), (wfl, ph))):
                        ins = nc.tensor.matmul(YB[m][:, 0:GT], w[:, j, c], h[:, j % 2, :],
                                               start=(j == 0 and i == 0), stop=(j == HT - 1 and i == 2))
                ins.then_inc(y_mm, 1)

            pe.wait_ge(w_lo, len(parts) // 2)
            product(0, 0, 0)
            with pe.Fori(0, NG // 2) as pair:
                for odd in range(2):
                    g = 2 * pair + odd
                    for j in range(HT):
                        if j == HT // 2 - 1:
                            pe.wait_ge(w_lo, len(parts))
                        if j < HT - 1:
                            product(g, j + 1, odd)
                        else:
                            pe.wait_ge(ln.lo_done, (g + 2) * KT)
                            product(g + 1, 0, 1 - odd)
                        if j == 0:
                            pe.wait_ge(wf_lo, 1)
                        output(g, j)
                        if j == HT // 2:
                            pe.wait_ge(x_done, 2 * g)
                            ln.pe_turn(nc, pe, k, g + 1, TB)
                    pe.wait_ge(ln.full_done, (g + 2) * KT)
                    pe.wait_ge(yT_done, (g + 1) * KT)
                    for b in range(GB):
                        for m in range(KT):
                            ins = nc.tensor.transpose(TB[b // 2][0:N, (b % 2) * D + 128 * m:(b % 2) * D + 128 * (m + 1)],
                                                      yT[:, m, b * N:(b + 1) * N], k.ident[:, :])
                        ins.then_inc(y_turned, 1)


def narrow_attention(nc, k, a, nxt):
    with ExitStack() as ctx:
        sb = lambda name, shape, dt=F32: ctx.enter_context(nc.sbuf_tensor("D_" + name, shape, dt))
        sem = phase_semaphores(k, 1)
        MT, SLOTS = H // 4, 2 * D
        wqh, wkh = [sb(f"w{w}_hi", [128, 2, SLOTS], F32R) for w in "qk"]
        wql, wkl = [sb(f"w{w}_lo", [128, 2, SLOTS], F32R) for w in "qk"]
        wvh, wvl = sb("wv_hi", [128, 2, D], F32R), sb("wv_lo", [128, 2, D], F32R)
        wo = sb("wo", [128, MT, D])
        ln = LN(nc, sb, sem, "", k.x, None, None, norm=False)
        lowhalf, bq, bk, bv = k.consts[:, 0:1], k.consts[:, 45:49], k.consts[:, 49:53], k.consts[:, 53:57]
        cx = Context(sb, sem, k.ctx_raw, k.first_ctx_in[1])
        qg = sb("q_group", [128, MT, GT])
        qh = sb("q_hi", [128, MT, N], F32R)
        ql = sb("q_lo", [128, MT, N], F32R)
        kf = sb("k_full", [128, SP])
        kr = sb("k_rounded", [128, SP], F32R)
        ks = sb("k_slots", [128, MT, SP], F32R)
        v = sb("v", [ST, 2, NS, H, 2, DL])
        P = sb("probs", [N, PS, 2, SP])
        bqs = sb("bq_scaled", [128, MT])
        PT = sb("probsT", [ST, 2, 2, NS, N])
        oT = sb("oT", [128, MT, N])
        nm = sb("neg_max", [N, PS, 2])
        sm = sb("sums", [N, PS, 2])
        rc = sb("rsums", [N, PS, 2])
        SB, TB, OB, YB, PJ = k.bank[0:2], k.bank[2:4], k.bank[4], k.bank[5], k.bank[6:8]

        wo_in, w_hi, w_lo, init, wo_cleared = sem("wo_in"), sem("w_hi"), sem("w_lo"), sem("init"), sem("wo_cleared")
        q_mm, q_act, q_dve, qh_done, ql_done = sem("q_mm"), sem("q_act"), sem("q_dve"), sem("qh"), sem("ql")
        k_mm, k_full, k_round, k_lo = sem("k_mm"), sem("k_full_done"), sem("k_rounded_done"), sem("k_slots_done")
        v_mm, v_out = sem("v_mm"), sem("v_out")
        s_done, max_done, exp_done = sem("scores_done"), sem("max_done"), sem("exp_done")
        rcp_done, norm_done, t_done = sem("rcp_done"), sem("norm_done"), sem("turned")
        pt_out, av_done, o_out = sem("probsT_out"), sem("av_done"), sem("oT_out")
        y_half, y_done, y_out = sem("y_half_done"), sem("y_done"), sem("y_out")
        x_done, bqs_set = sem("x_done"), sem("bq_scaled")
        KEYS = {0: 1, 1: 2, 2: 3}
        EXP0, NORM0, T0, PT0, AV0, O0, Y0 = 2, NP - 1, PS + NP - LAG, 2 * (1 + NP - LAG), 2 + NP - LAG - 1, 2 * (1 + 1), 1

        block = ctx.enter_context(nc.Block(no_gpsimd_drain=True))

        @block.sync
        def _(sp):
            wos = a["L1_xattn_Wo"].rearrange("(m s d) n -> s d m n", s=4, d=DL)
            sp.wait_ge(wo_cleared, 1)
            for s in range(4):
                sp.dma_start(wo[32 * s:32 * s + DL, :, :], wos[s, :, :, :]).then_inc(wo_in, 16)
            nxt(sp)
            clear_semaphores(sp, k, 0)
            cx.sp_loop(sp, a["ctx_768"])
            sp.wait_ge(ln.lo_done, (NG + 1) * KT)

        @block.gpsimd
        def _(pool):
            nc.gpsimd.memset(wo[:, :, :], 0.0).then_inc(wo_cleared, 1)
            nc.gpsimd.memset(k.y[:, 1 + B:1 + B + GB, :], 0.0).then_inc(k.ypad_set, 1)
            nc.gpsimd.memset(P[:, :, :, :], 0.0).then_inc(init, 1)
            nc.gpsimd.memset(PT[:, :, :, :, :].rearrange("p r j s n -> p (r j s n)"), 0.0).then_inc(init, 1)
            nc.gpsimd.memset(oT[:, :, :], 0.0).then_inc(init, 1)
            nc.gpsimd.memset(v[:, 1, :, :, :, :].rearrange("p s h r d -> p (s h r d)"), 0.0).then_inc(init, 1)
            with pool.Fori(0, NG) as g:
                for b in range(GB):
                    t = g * GB + b
                    pool.wait_ge(q_act, (g + 1) * (MT // 2))
                    pool.wait_ge(q_dve, (g + 1) * (MT // 2))
                    for u in range(MT):
                        pool.wait_ge(s_done, 2 * (t * NP + 2 * u + 2))
                        nc.gpsimd.tensor_tensor(qh[:, u, :], qg[:, u, b * N:(b + 1) * N],
                                                k.ones[:, :].to_broadcast([128, N]), ALU.mult
                                                ).then_inc(qh_done, 1)
                        pool.wait_ge(qh_done, t * MT + u + 1)
                        nc.gpsimd.tensor_tensor(ql[:, u, :], qg[:, u, b * N:(b + 1) * N], f32(qh[:, u, :]),
                                                ALU.subtract).then_inc(ql_done, 1)
                ln.split(nc.gpsimd, k, g + 1)

        @block.scalar
        def _(act):
            raws = {w: k.stage[:, 2, 512 * i:512 * (i + 1)].rearrange("p (t n) -> p t n", t=2) for i, w in enumerate("qkv")}

            def twice(w):
                return raws[w].rearrange("p t (h d) -> p (t h) d", d=DL).unsqueeze(2).to_broadcast([128, 2 * H, 2, DL])

            cx.act_hi(nc, act, 0, k.bank[2:4])
            for i, (w, src) in enumerate(((wkh, "k"), (wqh, "q"))):
                act.wait_ge(k.w_in[f"L1_xattn_W{src}"], (CONTEXT_LOADS, 16)[i])
                nc.scalar.activation(w[:, :, :].rearrange("p t (h r d) -> p (t h) r d", r=2, d=DL), twice(src), ACT.Copy
                                     ).then_inc(w_hi, 1)
            act.wait_ge(k.w_in["L1_xattn_Wv"], CONTEXT_LOADS)
            nc.scalar.activation(wvh[:, :, :], raws["v"], ACT.Copy).then_inc(w_hi, 1)
            ln.act_full(nc, act, 0, PJ)
            ln.act_round(nc, act, 0)
            act.sem_inc(o_out, O0)
            act.sem_inc(exp_done, EXP0)
            act.sem_inc(pt_out, PT0)

            def exps(t, u):
                act.wait_ge(t_done, (t + 1) * NP + u + 1)
                for j in range(2):
                    act.wait_ge(max_done, 2 * (t * NP + u) + j + 1)
                    nc.scalar.activation(P[:, u % PS, j, 0:S], SB[j][0:N, 0:S], ACT.Exp, bias=nm[:, u % PS, j:j + 1],
                                         accum_out=sm[:, u % PS, j:j + 1]).then_inc(exp_done, 1)

            def pt_evac(t, u):
                act.wait_ge(t_done, PS + (t + 1) * NP + u + 1)
                act.wait_ge(av_done, (t + 1) * NP + u + 1)
                for j in range(2):
                    nc.scalar.activation(PT[:, u % 2, j, :, :].rearrange("p s n -> p (s n)"), TB[j][0:ST, 0:NS * N],
                                         ACT.Copy).then_inc(pt_out, 1)

            def o_evac(t, h):
                act.wait_ge(av_done, 2 + (t + 1) * NP + 4 * h + 4)
                act.wait_ge(y_done if h else y_half, t + 1)
                for m in range(2 * h, 2 * h + 2):
                    nc.scalar.activation(oT[:, m, :], OB[:, m * N:(m + 1) * N], ACT.Identity, bias=bv[:, m:m + 1]
                                         ).then_inc(o_out, 1)

            def keys(t, m):
                act.wait_ge(k_mm, t * MT + m + 1)
                act.wait_ge(k_lo, t * MT + m)
                nc.scalar.activation(kf[:, :], PJ[0][:, 0:SP], ACT.Identity, bias=bk[:, m:m + 1]).then_inc(k_full, 1)

            def new_values(t, s, odd):
                act.wait_ge(v_mm, t * NS + s + 1)
                src = PJ[1 - s % 2][0:ST, 0:D].rearrange("p (h d) -> p h d", d=DL).unsqueeze(2).to_broadcast([ST, H, 2, DL])
                nc.scalar.activation(v[:, odd, s, :, :, :], src, ACT.Copy).then_inc(v_out, 1)

            keys(0, 0)
            for s in range(NS):
                new_values(0, s, 0)
            act.wait_ge(bqs_set, 1)
            with act.Fori(0, NG) as g:
                for i in range(0, MT, 2):
                    act.wait_ge(q_mm, g * MT + i + 1)
                    act.wait_ge(ql_done, g * GB * MT)
                    nc.scalar.activation(qg[:, i, :], PJ[0][:, 0:GT], ACT.Identity, bias=bqs[:, i:i + 1],
                                         scale=DL ** -0.5).then_inc(q_act, 1)
                ln.act_full(nc, act, g + 1, PJ)
                with act.Fori(0, GB // 2) as pair:
                    for odd in range(2):
                        t = g * GB + 2 * pair + odd
                        for u in range(NP):
                            pt_evac(t if u >= LAG else t - 1, (u - LAG) % NP)
                            if u == LAG:
                                o_evac(t - 1, 1)
                            if u == NP - 1:
                                o_evac(t, 0)
                            if u == LAG:
                                cx.act_hi(nc, act, t + 1, (PJ[1], YB))
                            exps(t, u)
                            if u in KEYS:
                                keys(t, KEYS[u])
                            if 0 < u - LAG <= NS:
                                new_values(t + 1, u - LAG - 1, 1 - odd)
                            if u == NP - 2:
                                keys(t + 1, 0)
            for u in range(NP - LAG, NP):
                pt_evac(B - 1, u)
            o_evac(B - 1, 1)

        @block.vector
        def _(dve):
            dve.sem_inc(y_out, Y0)
            dve.sem_inc(norm_done, NORM0)
            nc.vector.tensor_scalar(bqs[:, :], bq, DL ** -0.5, None, ALU.mult).then_inc(bqs_set, 1)
            for b in range(GB):
                ln.dve_norm(nc, dve, 0, b, True)
            cx.dve_lo(nc, dve, 0, k.bank[2:4])
            for w in (wkl, wvl):
                nc.vector.memset(f32(w[CR:128, 1, :]), 0.0).then_inc(init, 1)
            nc.vector.memset(OB[:, 0:4 * N], 0.0).then_inc(init, 1)
            nc.vector.memset(sm[:, PS - 1, :], 1.0).then_inc(init, 1)
            raws = {w: k.stage[:, 2, 512 * i:512 * (i + 1)].rearrange("p (t n) -> p t n", t=2) for i, w in enumerate("qkv")}
            for i, (w, wh, src, rows) in enumerate(((wkl, wkh, "k", CR), (wql, wqh, "q", 128), (wvl, wvh, "v", CR))):
                dve.wait_ge(w_hi, i + 1)
                for t, r in ((0, 128), (1, rows)):
                    if src == "v":
                        ins = nc.vector.tensor_tensor(w[0:r, t, :], raws[src][0:r, t, :], f32(wh[0:r, t, :]), ALU.subtract)
                    else:
                        raw = raws[src][0:r, t, :].rearrange("p (h d) -> p h d", d=DL)
                        slots = lambda x: x[0:r, t, :].rearrange("p (h r d) -> p h r d", r=2, d=DL)
                        for twice in range(2):
                            ins = nc.vector.tensor_tensor(slots(w)[:, :, twice, :], raw, f32(slots(wh)[:, :, twice, :]),
                                                          ALU.subtract)
                    ins.then_inc(w_lo, 1)
                if i == 1:
                    ln.dve_rest(nc, dve, 0)
            dve.wait_ge(init, 8)

            def maxima(t, u):
                for j in range(2):
                    dve.wait_ge(s_done, 2 * (NP + t * NP + u) + j + 1)
                    nc.vector.tensor_reduce(nm[:, u % PS, j:j + 1], SB[j][0:N, 0:S], AX.X, ALU.max, negate=True
                                            ).then_inc(max_done, 1)

            def norm(t, u):
                dve.wait_ge(exp_done, EXP0 + t * 2 * NP + 2 * u + 2)
                nc.vector.reciprocal(rc[:, u % PS, :], sm[:, u % PS, :]).then_inc(rcp_done, 1)
                dve.wait_ge(rcp_done, t * NP + u + 2)
                for j in range(2):
                    ins = nc.vector.tensor_scalar(P[:, u % PS, j, 0:S], P[:, u % PS, j, 0:S],
                                                  rc[:, u % PS, j:j + 1], None, ALU.mult)
                ins.then_inc(norm_done, 1)

            def keys(t, m):
                dve.wait_ge(k_full, t * MT + m + 1)
                nc.vector.tensor_copy(kr[:, :], kf[:, :]).then_inc(k_round, 1)
                dve.wait_ge(k_round, t * MT + m + 1)
                nc.vector.scalar_tensor_tensor(ks[:, m, :], f32(kr[:, :]), lowhalf, kf[:, :], ALU.mult, ALU.add
                                               ).then_inc(k_lo, 1)

            def x_update(t):
                dve.wait_ge(y_done, t + 2)
                dve.wait_ge(x_done, t + 1)
                yt = k.y[:, bass.ds(t + 1, 1), :].rearrange("p a d -> p (a d)")
                nc.vector.tensor_tensor(yt, YB[0:N, 0:D], k.bcast[:, 2, :], ALU.add).then_inc(y_out, 1)
                dve.wait_ge(y_out, Y0 + t + 2)
                xt = k.x[:, bass.ds(t + 1, 1), :].rearrange("p a d -> p (a d)")
                nc.vector.tensor_tensor(xt, xt, yt, ALU.add).then_inc(x_done, 1)

            keys(0, 0)
            with dve.Fori(0, NG) as g:
                for i in range(MT):
                    ln.dve_norm(nc, dve, g + 1, i)
                    if i % 2:
                        dve.wait_ge(q_mm, g * MT + i + 1)
                        dve.wait_ge(ql_done, g * GB * MT)
                        nc.vector.tensor_scalar(qg[:, i, :], PJ[1][:, 0:GT], bq[:, i:i + 1], DL ** -0.5, ALU.add,
                                                ALU.mult).then_inc(q_dve, 1)
                with dve.Fori(0, GB) as b:
                    t = g * GB + b
                    for u in range(NP):
                        maxima(t, u)
                        norm(t if u else t - 1, (u - 1) % NP)
                        if u in KEYS:
                            keys(t, KEYS[u])
                        if u == LAG:
                            cx.dve_lo(nc, dve, t + 1, (PJ[1], YB))
                        if u == NP - 2:
                            keys(t + 1, 0)
                        if u == NP - 1:
                            x_update(t - 1)
            norm(B - 1, NP - 1)
            x_update(B - 1)

        @block.tensor
        def _(pe):
            cx.pe_turn(nc, pe, k, 0, k.bank[2:4])
            ln.pe_turn(nc, pe, k, 0, PJ)
            pe.sem_inc(t_done, T0)
            pe.sem_inc(av_done, AV0)
            pe.sem_inc(s_done, 2 * NP)
            pe.wait_ge(w_lo, 2)
            pe.wait_ge(cx.lo_done, 2)

            def keys(t, m):
                c = slice(128 * m, 128 * (m + 1))
                mm5(nc, PJ[0][:, 0:SP], ([wkh[:, i, c] for i in range(2)], [wkl[:, i, c] for i in range(2)]),
                    cx.cols(slice(0, SP)), False).then_inc(k_mm, 1)

            def new_values(t, s):
                mm5(nc, PJ[1 - s % 2][0:ST, 0:D], cx.cols(slice(ST * s, ST * (s + 1))),
                    ([wvh[:, i, :] for i in range(2)], [wvl[:, i, :] for i in range(2)]), True).then_inc(v_mm, 1)

            def scores(t, u):
                if u % 2 == 0:
                    pe.wait_ge(ql_done, t * MT + u // 2 + 1)
                    pe.wait_ge(k_lo, t * MT + u // 2 + 1)
                for i, x in enumerate((qh, ql)):
                    for j in range(2):
                        if i == 0:
                            pe.wait_ge(exp_done, 2 * (t * NP + u) + j + 1)
                        r = slice(32 * (2 * (u % 2) + j), 32 * (2 * (u % 2) + j) + 32)
                        ins = nc.tensor.matmul(SB[j][0:N, 0:SP], x[r, u // 2, :], ks[r, u // 2, :],
                                               start=(i == 0), stop=(i == 1), tile_position=(r.start, 0))
                        if i == 1:
                            ins.then_inc(s_done, 1)

            def turn(t, u):
                pe.wait_ge(norm_done, (t + 1) * NP + u + 1)
                pe.wait_ge(pt_out, 2 * ((t + 1) * NP + u + 1))
                for j in range(2):
                    for s in range(NS):
                        ins = nc.tensor.transpose(TB[j][0:ST, s * N:(s + 1) * N],
                                                  P[:, u % PS, j, ST * s:ST * (s + 1)], k.ident[0:N, 0:N])
                ins.then_inc(t_done, 1)

            def values(t, u, odd):
                pe.wait_ge(pt_out, 2 * (1 + (t + 1) * NP + u + 1))
                if u % 4 == 0:
                    pe.wait_ge(o_out, 2 * ((t + 1) * 2 + u // 4 + 1))
                    if u == 0:
                        pe.wait_ge(v_out, (t + 1) * NS)
                for s in range(NS):
                    for j in range(2):
                        h = 2 * u + j
                        r = 32 * (h % 4)
                        ins = nc.tensor.matmul(OB[r:r + 32, (h // 4) * N:(h // 4 + 1) * N],
                                               v[:, odd, s, h, :, :].rearrange("p r d -> p (r d)"), PT[:, u % 2, j, s, :],
                                               start=(s == 0), stop=(s == NS - 1), tile_position=(0, r))
                ins.then_inc(av_done, 1)

            def project(t, half):
                pe.wait_ge(o_out, 2 * (1 + 2 * (t + 2)) - 2 * (1 - half))
                if half == 0:
                    pe.wait_ge(y_out, t + 2)
                for m in range(2 * half, 2 * half + 2):
                    ins = nc.tensor.matmul(YB[0:N, 0:D], oT[:, m, :], wo[:, m, :], start=(m == 0), stop=(m == MT - 1))
                ins.then_inc((y_half, y_done)[half], 1)

            pe.wait_ge(ln.full_done, KT)
            keys(0, 0)
            pe.wait_ge(w_lo, 6)
            new_values(0, 0)
            pe.wait_ge(k_full, 1)
            new_values(0, 1)
            pe.wait_ge(v_out, 1)
            new_values(0, 2)
            pe.wait_ge(init, 8)
            pe.wait_ge(wo_in, 64)
            with pe.Fori(0, NG) as g:
                pe.wait_ge(ln.lo_done, (g + 1) * KT)
                pe.wait_ge(k_full, g * GB * MT + 1)
                pe.wait_ge(v_out, (g * GB + 1) * NS)
                for i in range(MT):
                    if i >= 2:
                        pe.wait_ge((q_act, q_dve)[i % 2], g * (MT // 2) + i // 2)
                    m = slice(128 * i, 128 * (i + 1))
                    mm3(nc, PJ[i % 2][:, 0:GT], lambda t: wqh[:, t, m], lambda t: wql[:, t, m],
                        lambda t: ln.hi[:, t, :], lambda t: ln.lo[:, t, :], KT).then_inc(q_mm, 1)
                pe.wait_ge(q_act, (g + 1) * (MT // 2))
                pe.wait_ge(q_dve, (g + 1) * (MT // 2))
                ln.pe_turn(nc, pe, k, g + 1, PJ)
                with pe.Fori(0, GB // 2) as pair:
                    for odd in range(2):
                        t = g * GB + 2 * pair + odd
                        for u in range(NP):
                            turn(t if u >= LAG else t - 1, (u - LAG) % NP)
                            values(t if u > LAG else t - 1, (u - LAG - 1) % NP, odd if u > LAG else 1 - odd)
                            scores(t, u)
                            if u == LAG:
                                pe.wait_ge(v_out, (t + 1) * NS)
                                pe.wait_ge(y_out, t + 1)
                                cx.pe_turn(nc, pe, k, t + 1, (PJ[1], YB))
                            if odd == 0 and u == 0:
                                pe.wait_ge(ln.full_done, (g + 2) * KT)
                            if u in KEYS:
                                pe.wait_ge(k_full, t * MT + KEYS[u])
                                keys(t, KEYS[u])
                            if 0 < u - LAG <= NS:
                                s = u - LAG - 1
                                if s == 0:
                                    pe.wait_ge(cx.lo_done, 2 * (t + 2))
                                if s == 2:
                                    pe.wait_ge(v_out, (t + 1) * NS + 1)
                                if s == 1:
                                    pe.wait_ge(k_full, t * MT + MT)
                                new_values(t + 1, s)
                                if s == 2:
                                    project(t - 1, 0)
                            if u == NP - 2:
                                pe.wait_ge(v_out, (t + 1) * NS + 2)
                                keys(t + 1, 0)
                            if u == NP - 1:
                                project(t - 1, 1)
            for i in range(LAG):
                turn(B - 1, NP - LAG + i)
                values(B - 1, NP - LAG - 1 + i, 1)
            values(B - 1, NP - 1, 1)
            for half in range(2):
                project(B - 1, half)


def program(nc, a, out):
    with ExitStack() as ctx:
        k = Core()
        resident(nc, ctx, k)
        k.shared = ({}, {})
        k.c_in, k.rows_in, k.out_done = k.sem("vectors_in"), k.sem("rows_in"), k.sem("out_done")
        k.x_in, k.w_in = [k.sem(f"x_in{i}") for i in range(2)], {w: k.sem(f"{w}_in") for w in WEIGHTS}
        k.half_set, k.ident_set, k.pad_set = k.sem("half_set"), k.sem("ident_set"), k.sem("pad_set")
        k.mask_set, k.cols_turned, k.cols_set = k.sem("mask_set"), k.sem("cols_turned"), k.sem("cols_set")
        k.ypad_set, k.ctx_cleared = k.sem("ypad_set"), k.sem("ctx_cleared")
        k.first_ctx_in = [k.sem(f"first_ctx_in{i}") for i in range(2)]

        def plain(sp, dst, name, sem):
            t = a[name].shape[0] // 128
            sp.dma_start(dst.rearrange("p (t n) -> p t n", t=t), a[name].rearrange("(t p) n -> p t n", p=128)
                         ).then_inc(sem, 16)

        stage = k.stage[:, :, :].rearrange("p w n -> p (w n)")

        def weights_b(sp):
            sp.wait_ge(k.ctx_cleared, 1)
            load_context(sp, k.ctx_raw, a["ctx_768"], 0, k.first_ctx_in[0])
            plain(sp, k.stage[:, 0, :], "L0_xattn_Wq2", k.w_in["L0_xattn_Wq2"])
            context_weights_in(sp, k.stage[:, 1, :], a["L0_xattn_Wk2"], k.w_in["L0_xattn_Wk2"])
            context_weights_in(sp, k.stage[:, 2, :], a["L0_xattn_Wv2"], k.w_in["L0_xattn_Wv2"])

        def weights_c(sp):
            plain(sp, stage[:, 0:4096], "L0_xattn_Wp", k.w_in["L0_xattn_Wp"])
            plain(sp, stage[:, 4096:6144], "L0_xattn_Wf", k.w_in["L0_xattn_Wf"])

        def weights_de(sp):
            load_context(sp, k.ctx_raw, a["ctx_768"], 0, k.first_ctx_in[1])
            plain(sp, stage[:, 4096:4608], "L1_xattn_Wq", k.w_in["L1_xattn_Wq"])
            context_weights_in(sp, stage[:, 4608:5120], a["L1_xattn_Wk"], k.w_in["L1_xattn_Wk"])
            context_weights_in(sp, stage[:, 5120:5632], a["L1_xattn_Wv"], k.w_in["L1_xattn_Wv"])
            plain(sp, stage[:, 0:2048], "L1_xattn_W1", k.w_in["L1_xattn_W1"])
            plain(sp, stage[:, 2048:4096], "L1_xattn_W2", k.w_in["L1_xattn_W2"])

        def cut(lo, hi, t):
            return stage[:, lo:hi].rearrange("p (t n) -> p t n", t=t)

        nothing = lambda sp: None
        self_attention(nc, k, a, weights_b)
        cross_attention(nc, k, a, weights_c)
        feed_forward(nc, k, a, weights_de, "C_", True, None, cut(0, 4096, KT), cut(4096, 6144, FF // 128),
                     "L0_xattn_Wp", "L0_xattn_Wf", (13, 29), k.x, k.consts[:, 9:11], k.consts[:, 11:13])
        with nc.sbuf_tensor("y_tokens", [N, 1 + B + GB, D], F32) as y:
            k.y = y
            narrow_attention(nc, k, a, nothing)
            feed_forward(nc, k, a, nothing, "E_", False, out, cut(0, 2048, KT), cut(2048, 4096, FF // 128),
                         "L1_xattn_W1", "L1_xattn_W2", (35, 43), k.y, k.consts[:, 31:33], k.consts[:, 33:35])


_INS = [
    'x', 'ctx_768', 'L0_xattn_Wq1', 'L0_xattn_Wk1', 'L0_xattn_Wv1', 'L0_xattn_Wo1', 'L0_xattn_bo1',
    'L0_xattn_Wq2', 'L0_xattn_Wk2', 'L0_xattn_Wv2', 'L0_xattn_Wo2', 'L0_xattn_bo2', 'L0_xattn_Wp',
    'L0_xattn_bp', 'L0_xattn_Wf', 'L0_xattn_bf', 'L0_xattn_g1', 'L0_xattn_b1', 'L0_xattn_g2', 'L0_xattn_b2',
    'L0_xattn_g3', 'L0_xattn_b3', 'L1_xattn_Wq', 'L1_xattn_bq', 'L1_xattn_Wk', 'L1_xattn_bk', 'L1_xattn_Wv',
    'L1_xattn_bv', 'L1_xattn_Wo', 'L1_xattn_bo', 'L1_xattn_ln_g', 'L1_xattn_ln_b', 'L1_xattn_W1',
    'L1_xattn_b1', 'L1_xattn_W2', 'L1_xattn_b2',
]
_OUTS = [((16, 112, 256), "float32")]


def kernel(**inputs):
    import numpy as _np
    import concourse.bacc as _bacc
    from concourse import mybir as _mybir
    from concourse.bass_utils import run_bass_kernel_spmd as _run

    nc = _bacc.Bacc("TRN2", target_bir_lowering=False, num_devices=1)
    arrays, args = {}, {}
    for name in _INS:
        x = _np.ascontiguousarray(inputs[name])
        arrays[f"in_{name}_dram"] = x
        args[name] = nc.dram_tensor(f"in_{name}_dram", x.shape, _mybir.dt.from_np(x.dtype), kind="ExternalInput").ap()
    shape, dtype = _OUTS[0]
    out = nc.dram_tensor("out_0_dram", shape, _mybir.dt.from_np(_np.dtype(dtype)), kind="ExternalOutput").ap()
    program(nc, args, out)
    r = _run(nc, [arrays], core_ids=[0])
    return r.results[0]["out_0_dram"]
```
